# Optimizing a Trainium2 kernel written in Bass

```python
import numpy as np
import jax
import jax.numpy as jnp

def _softmax(x, axis=-1):
    return jax.nn.softmax(x, axis=axis)

def _gelu(x):
    return jax.nn.gelu(x, approximate=True)

def _silu(x):
    return jax.nn.silu(x)

def _sigmoid(x):
    return jax.nn.sigmoid(x)

def _layernorm(x, axis=-1, eps=1e-05):
    m = jnp.mean(x, axis=axis, keepdims=True)
    v = jnp.var(x, axis=axis, keepdims=True)
    return (x - m) / jnp.sqrt(v + eps)

def _scatter_add(tgt, idx, src, axis=0):
    return tgt.at[idx].add(src)

def _segment_sum(src, seg, n):
    return jax.ops.segment_sum(src, seg, n)
kernel_name = 'mk_lm_tower_d2_tok_ids1024_r4_f5b028'

def setup_inputs(seed: int=0):
    np.random.seed(seed)
    _w = jnp.asarray

    def _rec_inputs():
        import jax
        import jax.numpy as jnp
        _rk = jax.random.key(seed)
        x = jax.random.randint(jax.random.fold_in(_rk, 1), (4, 512), 0, 12564, jnp.int32)
        return x
    x = _rec_inputs()

    def _L0_tok_setup():
        import jax, jax.numpy as jnp
        import numpy as np
        VOCAB = 50257
        DIM = 256
        PADDING_IDX = 0
        key = jax.random.key(seed)
        k_w, k_ids = jax.random.split(key)
        weight = jax.random.normal(k_w, (VOCAB, DIM), dtype=jnp.float32)
        weight = weight.at[PADDING_IDX].set(0.0)
        input_ids = jax.random.randint(k_ids, (16, 512), 0, VOCAB, dtype=jnp.int64)
        return {'weight': weight, 'input_ids': input_ids}
    _L0_tok_all = _L0_tok_setup()
    _L0_tok_in = {k: v for k, v in _L0_tok_all.items() if k in ('weight',)}
    del _L0_tok_all

    def _L0_attn_setup():
        import jax, jax.numpy as jnp
        import numpy as np
        EPS = 1e-12
        key = jax.random.key(seed)
        k1, k2 = jax.random.split(key)
        b, n, d = (4, 1024, 256)
        x = jax.random.normal(k1, (b, n, d), dtype=jnp.float32)
        W_qkva = jax.random.normal(k2, (3 * d, d), dtype=jnp.float32) * 0.02
        gamma = jnp.ones((d,), dtype=jnp.float32)
        return {'x': x, 'W_qkva': W_qkva, 'gamma': gamma}
    _L0_attn_all = _L0_attn_setup()
    _L0_attn_in = {k: v for k, v in _L0_attn_all.items() if k in ('W_qkva', 'gamma')}
    del _L0_attn_all

    def _L0_ffn_setup():
        import jax, jax.numpy as jnp
        import numpy as np
        LATENT = 256
        LEAF_W = 64
        DEPTH = 4
        N_LEAVES = 2 ** DEPTH
        N_NODES = 2 ** DEPTH - 1
        B, S = (4, 512)

        def _fff_params(key, prefix):
            ks = jax.random.split(key, 4)
            d, h, l, n = (LATENT, LEAF_W, N_LEAVES, N_NODES)
            s_in = 1.0 / np.sqrt(d).astype(np.float32)
            s_h = 1.0 / np.sqrt(h).astype(np.float32)
            return {f'{prefix}_node_w': jax.random.normal(ks[0], (n, d), jnp.float32) * s_in, f'{prefix}_node_b': jax.random.normal(ks[1], (n,), jnp.float32) * s_in, f'{prefix}_w1': jax.random.normal(ks[2], (l, d, h), jnp.float32) * s_in, f'{prefix}_b1': jnp.zeros((l, h), jnp.float32), f'{prefix}_w2': jax.random.normal(ks[3], (l, h, d), jnp.float32) * s_h, f'{prefix}_b2': jnp.zeros((l, d), jnp.float32)}

        def _fff(x, node_w, node_b, w1, b1, w2, b2):
            Bx, Sx, D = x.shape
            xf = x.reshape(-1, D)
            N = xf.shape[0]
            cur = jnp.zeros((N,), jnp.int32)
            for _ in range(DEPTH):
                pw = node_w[cur]
                score = jnp.einsum('nd,nd->n', xf, pw) + node_b[cur]
                cur = 2 * cur + 1 + (score >= 0).astype(jnp.int32)
            leaf = cur - N_NODES
            sel = jax.nn.one_hot(leaf, N_LEAVES, dtype=xf.dtype)
            hidden_all = jax.nn.relu(jnp.einsum('nd,ldh->lnh', xf, w1) + b1[:, None, :])
            hidden = hidden_all * sel.T[:, :, None]
            out = jnp.einsum('lnh,lho->no', hidden, w2) + sel @ b2
            return out.reshape(Bx, Sx, D)
        key = jax.random.key(seed)
        kx, kq, kk, kv = jax.random.split(key, 4)
        inp = {'x': jax.random.normal(kx, (B, S, LATENT), jnp.float32)}
        inp.update(_fff_params(kq, 'q'))
        inp.update(_fff_params(kk, 'k'))
        inp.update(_fff_params(kv, 'v'))
        return inp
    _L0_ffn_all = _L0_ffn_setup()
    _L0_ffn_in = {k: v for k, v in _L0_ffn_all.items() if k in ('q_node_w', 'q_node_b', 'q_w1', 'q_b1', 'q_w2', 'q_b2', 'k_node_w', 'k_node_b', 'k_w1', 'k_b1', 'k_w2', 'k_b2', 'v_node_w', 'v_node_b', 'v_w1', 'v_b1', 'v_w2', 'v_b2')}
    del _L0_ffn_all

    def _L1_attn_setup():
        import jax, jax.numpy as jnp
        import numpy as np
        H, HD, D = (16, 64, 256)
        SCALE = HD ** (-0.5)
        TEMP = 1.0
        EPS = 1e-05
        key = jax.random.key(seed)
        ks = jax.random.split(key, 10)
        B, N = (2, 512)
        lim = 1.0 / np.sqrt(D)

        def lin(k, out_d, in_d):
            k1, k2 = jax.random.split(k)
            W = jax.random.uniform(k1, (out_d, in_d), jnp.float32, -lim, lim)
            b = jax.random.uniform(k2, (out_d,), jnp.float32, -lim, lim)
            return (W, b)
        Wq, bq = lin(ks[0], H * HD, D)
        Wk, bk = lin(ks[1], H * HD, D)
        Wv, bv = lin(ks[2], H * HD, D)
        Wo, bo = lin(ks[3], D, H * HD)
        return {'x': jax.random.normal(ks[4], (B, N, D), jnp.float32), 'adaptive_scale': jnp.ones((H,), jnp.float32), 'Wq': Wq, 'bq': bq, 'Wk': Wk, 'bk': bk, 'Wv': Wv, 'bv': bv, 'Wo': Wo, 'bo': bo, 'gamma': jnp.ones((D,), jnp.float32), 'beta': jnp.zeros((D,), jnp.float32)}
    _L1_attn_all = _L1_attn_setup()
    _L1_attn_in = {k: v for k, v in _L1_attn_all.items() if k in ('adaptive_scale', 'Wq', 'bq', 'Wk', 'bk', 'Wv', 'bv', 'Wo', 'bo', 'gamma', 'beta')}
    del _L1_attn_all

    def _L1_ffn_setup():
        import jax, jax.numpy as jnp
        import numpy as np
        BLOCK = 16
        _GRID = jnp.array([0.0, 0.5, 1.0, 1.5, 2.0, 3.0, 4.0, 6.0], dtype=jnp.float32)
        _MID = jnp.array([0.25, 0.75, 1.25, 1.75, 2.5, 3.5, 5.0], dtype=jnp.float32)

        def fp4_quant_dequant(x):
            shape = x.shape
            xb = x.reshape(shape[:-1] + (shape[-1] // BLOCK, BLOCK))
            scale = jnp.max(jnp.abs(xb), axis=-1, keepdims=True) / 6.0
            scale = jnp.maximum(scale, jnp.float32(1e-12))
            xn = xb / scale
            idx = jnp.searchsorted(_MID, jnp.abs(xn))
            q = _GRID[idx] * jnp.sign(xn) * scale
            return q.reshape(shape)

        def fp4_linear(x, w):
            xq = fp4_quant_dequant(x)
            wq = fp4_quant_dequant(w)
            return jnp.einsum('bsk,nk->bsn', xq, wq)
        key = jax.random.key(seed)
        k1, k2, k3, k4 = jax.random.split(key, 4)
        H, I = (256, 704)
        x = jax.random.normal(k1, (4, 1024, H), dtype=jnp.float32)
        w_gate = jax.random.normal(k2, (I, H), dtype=jnp.float32) * 0.02
        w_up = jax.random.normal(k3, (I, H), dtype=jnp.float32) * 0.02
        w_down = jax.random.normal(k4, (H, I), dtype=jnp.float32) * 0.02
        return {'x': x, 'w_gate': w_gate, 'w_up': w_up, 'w_down': w_down}
    _L1_ffn_all = _L1_ffn_setup()
    _L1_ffn_in = {k: v for k, v in _L1_ffn_all.items() if k in ('w_gate', 'w_up', 'w_down')}
    del _L1_ffn_all
    return {'x': x, 'L0_tok_weight': _L0_tok_in['weight'], 'L0_attn_W_qkva': _L0_attn_in['W_qkva'], 'L0_attn_gamma': _L0_attn_in['gamma'], 'L0_ffn_q_node_w': _L0_ffn_in['q_node_w'], 'L0_ffn_q_node_b': _L0_ffn_in['q_node_b'], 'L0_ffn_q_w1': _L0_ffn_in['q_w1'], 'L0_ffn_q_b1': _L0_ffn_in['q_b1'], 'L0_ffn_q_w2': _L0_ffn_in['q_w2'], 'L0_ffn_q_b2': _L0_ffn_in['q_b2'], 'L0_ffn_k_node_w': _L0_ffn_in['k_node_w'], 'L0_ffn_k_node_b': _L0_ffn_in['k_node_b'], 'L0_ffn_k_w1': _L0_ffn_in['k_w1'], 'L0_ffn_k_b1': _L0_ffn_in['k_b1'], 'L0_ffn_k_w2': _L0_ffn_in['k_w2'], 'L0_ffn_k_b2': _L0_ffn_in['k_b2'], 'L0_ffn_v_node_w': _L0_ffn_in['v_node_w'], 'L0_ffn_v_node_b': _L0_ffn_in['v_node_b'], 'L0_ffn_v_w1': _L0_ffn_in['v_w1'], 'L0_ffn_v_b1': _L0_ffn_in['v_b1'], 'L0_ffn_v_w2': _L0_ffn_in['v_w2'], 'L0_ffn_v_b2': _L0_ffn_in['v_b2'], 'L1_attn_adaptive_scale': _L1_attn_in['adaptive_scale'], 'L1_attn_Wq': _L1_attn_in['Wq'], 'L1_attn_bq': _L1_attn_in['bq'], 'L1_attn_Wk': _L1_attn_in['Wk'], 'L1_attn_bk': _L1_attn_in['bk'], 'L1_attn_Wv': _L1_attn_in['Wv'], 'L1_attn_bv': _L1_attn_in['bv'], 'L1_attn_Wo': _L1_attn_in['Wo'], 'L1_attn_bo': _L1_attn_in['bo'], 'L1_attn_gamma': _L1_attn_in['gamma'], 'L1_attn_beta': _L1_attn_in['beta'], 'L1_ffn_w_gate': _L1_ffn_in['w_gate'], 'L1_ffn_w_up': _L1_ffn_in['w_up'], 'L1_ffn_w_down': _L1_ffn_in['w_down']}

def reference(x, L0_tok_weight, L0_attn_W_qkva, L0_attn_gamma, L0_ffn_q_node_w, L0_ffn_q_node_b, L0_ffn_q_w1, L0_ffn_q_b1, L0_ffn_q_w2, L0_ffn_q_b2, L0_ffn_k_node_w, L0_ffn_k_node_b, L0_ffn_k_w1, L0_ffn_k_b1, L0_ffn_k_w2, L0_ffn_k_b2, L0_ffn_v_node_w, L0_ffn_v_node_b, L0_ffn_v_w1, L0_ffn_v_b1, L0_ffn_v_w2, L0_ffn_v_b2, L1_attn_adaptive_scale, L1_attn_Wq, L1_attn_bq, L1_attn_Wk, L1_attn_bk, L1_attn_Wv, L1_attn_bv, L1_attn_Wo, L1_attn_bo, L1_attn_gamma, L1_attn_beta, L1_ffn_w_gate, L1_ffn_w_up, L1_ffn_w_down):
    import jax
    import jax.numpy as jnp

    def _L0_tok_ref(weight, input_ids):
        import jax, jax.numpy as jnp
        import numpy as np
        VOCAB = 50257
        DIM = 256
        PADDING_IDX = 0
        return jnp.take(weight, input_ids, axis=0)

    def _L0_attn_ref(x, W_qkva, gamma):
        import jax, jax.numpy as jnp
        import numpy as np
        EPS = 1e-12
        d = gamma.shape[0]
        scale = d ** 0.5
        norm = jnp.maximum(jnp.linalg.norm(x, axis=-1, keepdims=True), EPS)
        xn = x / norm * scale * gamma
        h = jnp.einsum('bnd,ed->bne', xn, W_qkva)
        q, kv, a = jnp.split(h, 3, axis=-1)
        a = jax.nn.sigmoid(a)

        def binop(e_i, e_j):
            a_i, kv_i = e_i
            a_j, kv_j = e_j
            return (a_j * a_i, a_j * kv_i + kv_j)
        _, y = jax.lax.associative_scan(binop, (a, kv), axis=1)
        return q * y

    def _L0_ffn_ref(x, q_node_w, q_node_b, q_w1, q_b1, q_w2, q_b2, k_node_w, k_node_b, k_w1, k_b1, k_w2, k_b2, v_node_w, v_node_b, v_w1, v_b1, v_w2, v_b2):
        import jax, jax.numpy as jnp
        import numpy as np
        LATENT = 256
        LEAF_W = 64
        DEPTH = 4
        N_LEAVES = 2 ** DEPTH
        N_NODES = 2 ** DEPTH - 1
        B, S = (4, 512)

        def _fff_params(key, prefix):
            ks = jax.random.split(key, 4)
            d, h, l, n = (LATENT, LEAF_W, N_LEAVES, N_NODES)
            s_in = 1.0 / np.sqrt(d).astype(np.float32)
            s_h = 1.0 / np.sqrt(h).astype(np.float32)
            return {f'{prefix}_node_w': jax.random.normal(ks[0], (n, d), jnp.float32) * s_in, f'{prefix}_node_b': jax.random.normal(ks[1], (n,), jnp.float32) * s_in, f'{prefix}_w1': jax.random.normal(ks[2], (l, d, h), jnp.float32) * s_in, f'{prefix}_b1': jnp.zeros((l, h), jnp.float32), f'{prefix}_w2': jax.random.normal(ks[3], (l, h, d), jnp.float32) * s_h, f'{prefix}_b2': jnp.zeros((l, d), jnp.float32)}

        def _fff(x, node_w, node_b, w1, b1, w2, b2):
            Bx, Sx, D = x.shape
            xf = x.reshape(-1, D)
            N = xf.shape[0]
            cur = jnp.zeros((N,), jnp.int32)
            for _ in range(DEPTH):
                pw = node_w[cur]
                score = jnp.einsum('nd,nd->n', xf, pw) + node_b[cur]
                cur = 2 * cur + 1 + (score >= 0).astype(jnp.int32)
            leaf = cur - N_NODES
            sel = jax.nn.one_hot(leaf, N_LEAVES, dtype=xf.dtype)
            hidden_all = jax.nn.relu(jnp.einsum('nd,ldh->lnh', xf, w1) + b1[:, None, :])
            hidden = hidden_all * sel.T[:, :, None]
            out = jnp.einsum('lnh,lho->no', hidden, w2) + sel @ b2
            return out.reshape(Bx, Sx, D)
        q = _fff(x, q_node_w, q_node_b, q_w1, q_b1, q_w2, q_b2)
        k = _fff(x, k_node_w, k_node_b, k_w1, k_b1, k_w2, k_b2)
        v = _fff(x, v_node_w, v_node_b, v_w1, v_b1, v_w2, v_b2)
        scale = 1.0 / np.sqrt(LATENT).astype(np.float32)
        attn = jax.nn.softmax(jnp.einsum('bqd,bkd->bqk', q, k) * scale, axis=-1)
        return jnp.einsum('bqk,bkd->bqd', attn, v)

    def _L1_attn_ref(x, adaptive_scale, Wq, bq, Wk, bk, Wv, bv, Wo, bo, gamma, beta):
        import jax, jax.numpy as jnp
        import numpy as np
        H, HD, D = (16, 64, 256)
        SCALE = HD ** (-0.5)
        TEMP = 1.0
        EPS = 1e-05
        B, N, _ = x.shape
        Q = (x @ Wq.T + bq).reshape(B, N, H, HD)
        K = (x @ Wk.T + bk).reshape(B, N, H, HD)
        V = (x @ Wv.T + bv).reshape(B, N, H, HD)
        scores = jnp.einsum('bnhd,bmhd->bhnm', Q, K)
        scores = scores * (SCALE * adaptive_scale)[None, :, None, None] / TEMP
        w = jax.nn.softmax(scores, axis=-1)
        attn = jnp.einsum('bhnm,bmhd->bnhd', w, V).reshape(B, N, H * HD)
        y = x + (attn @ Wo.T + bo)
        mu = jnp.mean(y, axis=-1, keepdims=True)
        var = jnp.var(y, axis=-1, keepdims=True)
        return (y - mu) / jnp.sqrt(var + EPS) * gamma + beta

    def _L1_ffn_ref(x, w_gate, w_up, w_down):
        import jax, jax.numpy as jnp
        import numpy as np
        BLOCK = 16
        _GRID = jnp.array([0.0, 0.5, 1.0, 1.5, 2.0, 3.0, 4.0, 6.0], dtype=jnp.float32)
        _MID = jnp.array([0.25, 0.75, 1.25, 1.75, 2.5, 3.5, 5.0], dtype=jnp.float32)

        def fp4_quant_dequant(x):
            shape = x.shape
            xb = x.reshape(shape[:-1] + (shape[-1] // BLOCK, BLOCK))
            scale = jnp.max(jnp.abs(xb), axis=-1, keepdims=True) / 6.0
            scale = jnp.maximum(scale, jnp.float32(1e-12))
            xn = xb / scale
            idx = jnp.searchsorted(_MID, jnp.abs(xn))
            q = _GRID[idx] * jnp.sign(xn) * scale
            return q.reshape(shape)

        def fp4_linear(x, w):
            xq = fp4_quant_dequant(x)
            wq = fp4_quant_dequant(w)
            return jnp.einsum('bsk,nk->bsn', xq, wq)
        gate = fp4_linear(x, w_gate)
        y = fp4_linear(x, w_up)
        h = jax.nn.silu(gate) * y
        return fp4_linear(h, w_down)
    h = _L0_tok_ref(L0_tok_weight, x)
    h = h + _L0_attn_ref(_layernorm(h, axis=-1), L0_attn_W_qkva, L0_attn_gamma)
    h = h + _L0_ffn_ref(_layernorm(h, axis=-1), L0_ffn_q_node_w, L0_ffn_q_node_b, L0_ffn_q_w1, L0_ffn_q_b1, L0_ffn_q_w2, L0_ffn_q_b2, L0_ffn_k_node_w, L0_ffn_k_node_b, L0_ffn_k_w1, L0_ffn_k_b1, L0_ffn_k_w2, L0_ffn_k_b2, L0_ffn_v_node_w, L0_ffn_v_node_b, L0_ffn_v_w1, L0_ffn_v_b1, L0_ffn_v_w2, L0_ffn_v_b2)
    h = h + _L1_attn_ref(_layernorm(h, axis=-1), L1_attn_adaptive_scale, L1_attn_Wq, L1_attn_bq, L1_attn_Wk, L1_attn_bk, L1_attn_Wv, L1_attn_bv, L1_attn_Wo, L1_attn_bo, L1_attn_gamma, L1_attn_beta)
    h = h + _L1_ffn_ref(_layernorm(h, axis=-1), L1_ffn_w_gate, L1_ffn_w_up, L1_ffn_w_down)
    return h

_drawn_inputs = setup_inputs


def setup_inputs(seed=0):
    import zlib

    import numpy as np

    out = dict(_drawn_inputs(seed))
    spreads = {'L0_attn_gamma': (1.0, 0.2),
     'L0_ffn_q_b1': (0.0, 0.8),
     'L0_ffn_q_b2': (0.0, 0.8),
     'L0_ffn_k_b1': (0.0, 0.8),
     'L0_ffn_k_b2': (0.0, 0.8),
     'L0_ffn_v_b1': (0.0, 0.59),
     'L0_ffn_v_b2': (0.0, 0.294),
     'L1_attn_adaptive_scale': (1.0, 0.6),
     'L1_attn_gamma': (1.0, 0.2),
     'L1_attn_beta': (0.0, 0.1)}
    factors = {'L0_ffn_q_node_w': 3.358,
     'L0_ffn_q_node_b': 8.0,
     'L0_ffn_q_w1': 3.897,
     'L0_ffn_q_w2': 3.265,
     'L0_ffn_k_node_w': 3.268,
     'L0_ffn_k_node_b': 8.0,
     'L0_ffn_k_w1': 3.805,
     'L0_ffn_k_w2': 3.302,
     'L0_ffn_v_node_b': 3.46,
     'L1_attn_Wq': 5.576,
     'L1_attn_bq': 8.0,
     'L1_attn_Wk': 5.571,
     'L1_attn_bk': 8.0,
     'L1_attn_bo': 3.081,
     'L1_ffn_w_gate': 4.193,
     'L1_ffn_w_up': 4.154,
     'L1_ffn_w_down': 4.144}
    for name, (base, spread) in spreads.items():
        noise = np.random.default_rng([zlib.crc32(name.encode()), seed]).standard_normal(out[name].shape)
        drawn = base * np.exp(spread * noise) if base else spread * noise
        out[name] = jnp.asarray(drawn.astype(out[name].dtype))
    for name, factor in factors.items():
        out[name] = (out[name] * factor).astype(out[name].dtype)
    return out
```

```python
from contextlib import ExitStack

import concourse.bass as bass
from concourse import mybir

F32 = mybir.dt.float32
F32R = mybir.dt.float32r
U32 = mybir.dt.uint32
I32 = mybir.dt.int32
ALU = mybir.AluOpType
ACT = mybir.ActivationFunctionType
AX = mybir.AxisListType

P = 128
NSEQ, SEQ, D = 4, 512, 256
NBLK = SEQ // P
KD = D // P
SPLIT = 2

E1 = 3 * D
LEAVES, LEAFW, DEPTH = 16, 64, 4
NODES = LEAVES - 1
HID = LEAVES * LEAFW
NH2 = HID // P
TREE = 32
RT = 3 * TREE
NNODE = 48
FAR = 2.0 ** 120
HEADS, HDIM = 16, 64
PAIRS = HEADS // 2
QUARTERS = 4
UNITS = HEADS * NBLK
FF = 704
FPB = 16
NFB = FF // FPB
FK = (FF + P - 1) // P
FTAIL = FF - (FK - 1) * P
GRID_HALF = 0.75 * 2.0 ** 23
GRID_ONE = 1.5 * 2.0 ** 23
GRID_TWO = 3.0 * 2.0 ** 23
BELOW = 1.0 - 2.0 ** -23

CH = 512
NCH2 = 3 * 4 * 1024 // CH
NCH3 = 8 * 1024 // CH
LN_EPS = 1e-5


class Banks:

    def __init__(self, filled, emptied):
        self.filled_sem, self.emptied_sem = filled, emptied
        self.before = [0] * 8

    def layer(self, order):
        if hasattr(self, "place"):
            self.before = [n + NSEQ * k for n, k in zip(self.before, self.per)]
        self.place, self.per = {}, [0] * 8
        for what, bank in order:
            assert what not in self.place
            self.place[what] = (bank, self.per[bank])
            self.per[bank] += 1
        return BankLayer(self, dict(self.place), list(self.per), list(self.before))


class BankLayer:
    def __init__(self, banks, place, per, before):
        self.banks, self.place, self.per, self.before = banks, place, per, before

    def count(self, what, b, more):
        bank, n = self.place[what]
        return b * self.per[bank] + (self.before[bank] + n + more)

    def room(self, what, b):
        return self.banks.emptied_sem[self.place[what][0]], self.count(what, b, 1)

    def filled(self, what, b):
        return self.banks.filled_sem[self.place[what][0]], self.count(what, b, 1)

    def emptied(self, what, b):
        return self.banks.emptied_sem[self.place[what][0]], self.count(what, b, 2)

    def fill(self, what):
        return self.banks.filled_sem[self.place[what][0]]

    def empty(self, what):
        return self.banks.emptied_sem[self.place[what][0]]


class Steps:

    def __init__(self, sem):
        self.sem, self.base = sem, 0

    def start(self, b, per):
        self.b, self.per, self.n = b, per, 0

    def end(self):
        assert self.n == self.per, f"steps {self.n}, declared {self.per}"
        self.base += self.per * (NSEQ if self.per and not isinstance(self.b, int) else 1)

    def link(self, eng, ins):
        self.n += 1
        ins.then_inc(self.sem, 1)
        eng.wait_ge(self.sem, self.b * self.per + (self.base + self.n))


def unit_steps():
    steps = []
    for u in range(UNITS):
        pair, r = divmod(u, 2 * NBLK)
        todo = []
        if pair + 1 < PAIRS:
            if r == 0:
                todo.append(("Q", pair + 1))
            if r == 2:
                todo.append(("K", pair + 1))
            if pair % 2 and r in (4, 6):
                todo.append(("V", (pair + 1) // 2, (r - 4) // 2))
        if u + 2 < UNITS:
            todo.append(("S", u + 2))
        todo.append(("T", u))
        if u % 2 == 0 and u >= 2:
            todo.append(("PV", u // 2 - 1))
        if r == 5 and pair:
            todo.append(("O", pair - 1))
        steps += todo
    return ([("xT", k) for k in range(KD)] + [("Q", 0), ("K", 0), ("V", 0, 0), ("V", 0, 1), ("S", 0), ("S", 1)]
            + steps + [("PV", UNITS // 2 - 1), ("O", PAIRS - 1)])


def build(nc, ids, table, w1qkva, gamma1, node_w, node_b, w2raw, route, b1, b2, w3raw, bq, bk, bv,
          ascale_row, ascale_part, bo, gamma3, beta3, w_gate, w_up, w_down, ident_in, out):
    with ExitStack() as ctx:
        def region(name, cols, dt):
            return ctx.enter_context(nc.sbuf_tensor(name, [P, cols], dt))

        def sem(name):
            return ctx.enter_context(nc.semaphore(name))

        opnd = region("operands", 41472, F32R)
        data = region("data", 10240, F32)
        small = region("small", 600, F32)
        idx = region("token_ids", NSEQ * NBLK, I32)

        def cut(tensor, at, *shape):
            n = 1
            for s in shape:
                n *= s
            ap = tensor[:, at:at + n]
            names = "abcd"[:len(shape)]
            if len(shape) == 1:
                return ap
            return ap.rearrange(f"p ({' '.join(names)}) -> p {' '.join(names)}",
                                **{c: s for c, s in zip(names[1:], shape[1:])})

        def f32(ap):
            return ap.bitcast(F32)

        h = cut(data, 0, NSEQ * NBLK, D)
        xn = cut(data, 4096, NBLK, D)
        A0 = 5120
        raw = cut(data, A0 + 2048, 3, CH)
        gate = cut(data, A0, KD, SEQ)
        scan = cut(data, A0 + 1024, KD, SEQ)
        W2 = 0
        w2 = cut(opnd, W2, SPLIT, 3, 4, 1024)
        xT = cut(opnd, 24576, SPLIT, KD, SEQ)
        route_w = cut(opnd, 26624, 3, HID)
        b2w = cut(opnd, 29696, SPLIT, 3, D)
        selT = cut(opnd, 31232, 2, SEQ)
        hid = cut(opnd, 32256, 3, SPLIT, SEQ)
        qT = cut(opnd, 35328, SPLIT, KD, SEQ)
        kT = cut(opnd, 37376, SPLIT, KD, SEQ)
        v2 = cut(opnd, 39424, SPLIT, NBLK, D)
        pT2 = cut(opnd, 32256, 2, SPLIT, SEQ)
        w1 = cut(opnd, 35328, SPLIT, KD, E1)
        route_lo = cut(opnd, 39424, HID)
        p2 = cut(data, A0, 2, SEQ)
        sel = cut(data, A0 + 1024, NBLK, 2, RT)
        path = cut(data, A0 + 1024 + NBLK * 2 * RT, 3, NBLK, 3, 8)
        w3 = cut(opnd, 0, SPLIT, 8, 1024)
        qk = cut(opnd, 32256, 2, 2, SPLIT, SEQ)
        vs = cut(opnd, 36352, 2, NBLK, 4, P)
        pT3 = cut(opnd, 26624, 2, SPLIT, NBLK, D)
        at3 = (cut(opnd, 30720, SPLIT, SEQ), cut(opnd, 40448, SPLIT, SEQ))
        p3 = cut(data, A0, 2, SEQ)
        pn3 = cut(data, A0 + 1024, 2, SEQ)
        att = cut(data, A0 + 2048, SEQ)
        att_lo = cut(data, A0 + 2560, SEQ)
        rawl = cut(data, A0, 4, CH)
        y3 = cut(data, A0, NBLK, D)
        t3 = cut(data, A0 + 1024, NBLK, D)
        rows3 = cut(data, A0 + 3072, 3, D)
        wgu = cut(opnd, 0, SPLIT, KD, 2 * FF)
        wdn = cut(opnd, 5632, SPLIT, FK, D)
        hqT = cut(opnd, 8704, SPLIT, FK, P)
        FW = 768
        q_x = data[:, A0:A0 + FW]
        q_a = data[:, A0 + FW:A0 + 2 * FW]
        q_b = data[:, A0 + 2 * FW:A0 + 3 * FW]
        q_c = cut(data, A0 + 3 * FW, 2, FW)
        silu = data[:, A0 + 5 * FW:A0 + 5 * FW + FF]
        q_max = data[:, A0 + 4544:A0 + 4544 + FW // FPB]
        q_inv = data[:, A0 + 4592:A0 + 4592 + FW // FPB]

        ident = small[:, 0:128]
        stats = cut(small, 128, NBLK, 6)
        mv = cut(small, 152, NBLK, 2)
        var_e = small[:, 160:164]
        rstd = small[:, 164:168]
        sdev = small[:, 168:172]
        coef = small[:, 172:176]
        neg_half = small[:, 176:180]
        pos_half = small[:, 180:184]
        gam1 = small[:, 184:186]
        nodeb = small[:, 186:186 + 3 * NODES]
        nodew = cut(small, 240, KD, NNODE)
        score = cut(small, 336, NBLK, 3 * NODES)
        nmax = small[:, 520:524]
        rsum = small[:, 524:528]
        rinv = small[:, 528:532]
        bqs = small[:, 532:540]
        bks = small[:, 540:548]
        bvs = small[:, 548:564]
        asr = small[:, 564:580]
        asp = small[:, 580:588]
        nodeR = region("node_operands", SPLIT * KD * NNODE, F32R)
        noder = cut(nodeR, 0, SPLIT, KD, NNODE)

        bank = [ctx.enter_context(nc.psum_tensor(f"bank{k}", [P, 512], F32)) for k in range(8)]
        banks = Banks([sem(f"bank_filled{k}") for k in range(8)], [sem(f"bank_emptied{k}") for k in range(8)])

        L1 = banks.layer([(("xT", k), k) for k in range(KD)]
                         + [((n, c), 2 + 3 * c + m) for c in range(KD) for m, n in enumerate(("a", "kv", "q"))]
                         + [(("back", t), t) for t in range(2)])
        hid_bank = {(f, j): 5 + (NH2 * f + j) % 3 for f in range(3) for j in range(NH2)}
        order = [(("xT", k), k) for k in range(KD)] + [("node", 2), ("selT", 3), ("takT", 4)]
        for f in range(3):
            order += [(("hid", f, j), hid_bank[f, j]) for j in range(NH2)]
            order += [(("tree", f, o), o) for o in range(KD if f < 2 else NBLK)]
        for i in range(NBLK):
            order += [(("S", i), 4 + i % 2), (("T", i), 6 + i % 2), (("PV", i), i % 2)]
        L2 = banks.layer(order)
        STEPS3 = unit_steps()
        where3 = {"xT": lambda k: 4 + k, "Q": lambda p: 5, "K": lambda p: 5, "V": lambda q, t: 5, "S": lambda u: u % 2,
                  "T": lambda u: 2 + u % 2}
        order = []
        for s in STEPS3:
            if s[0] == "PV":
                if s[1] % 2 == 0:
                    order.append((("PV", s[1] // 2), 4))
            elif s[0] != "O":
                order.append((s, where3[s[0]](*s[1:])))
        L3 = banks.layer(order + [(("O", t), 6 + t) for t in range(2)])
        order = [(("xT", k), k) for k in range(KD)]
        for i in range(NBLK):
            order += [(("gate", i, t), 2 + t) for t in range(2)] + [(("up", i, t), 4 + t) for t in range(2)]
            order += [(("hT", i, t), 6 + t) for t in range(2)] + [(("down", i), i % 2)]
        L4 = banks.layer(order)

        ids_in = sem("ids_in")
        consts_in = sem("consts_in")
        rows_gathered = sem("rows_gathered")
        w1_in = sem("w1_in")
        route_in = sem("route_in")
        route_lo_moved = sem("route_lo_moved")
        raw_in = [sem(f"raw_in{s}") for s in range(4)]
        raw_hi = sem("raw_hi")
        raw_lo = sem("raw_lo")
        w1_ready = sem("w1_ready")
        setup_done = sem("setup_done")
        route_split = sem("route_split")
        var_ready = sem("var_ready")
        rstd_ready = sem("rstd_ready")
        xn_ready = sem("xn_ready")
        xhi_ready = sem("xhi_ready")
        gate_ready = sem("gate_ready")
        sel_ready = sem("sel_ready")
        hid_hi = sem("hid_hi")
        hid_used = sem("hid_used")
        tree_hi = sem("tree_hi")
        nmax_ready = sem("nmax_ready")
        p_hi = sem("p_hi")
        dve_step = sem("dve_step")
        pool_step = sem("pool_step")
        w3_prepared = sem("w3_prepared")
        rows3_in = sem("rows3_in")
        proj_hi = sem("proj_hi")
        rinv_ready = sem("rinv_ready")
        pn_ready = sem("pn_ready")
        att_shift = sem("att_shift")
        att_ready = sem("att_ready")
        att_hi = sem("att_hi")
        at_ready = sem("at_ready")
        w3_prepared_q = sem("w3_prepared_q")
        w3_hi = sem("w3_hi")
        coef_ready = sem("coef_ready")
        h3_done = sem("h3_done")
        w4_in = sem("w4_in")
        w4_abs = sem("w4_abs")
        w4_quantized = sem("w4_quantized")
        w4_turned = sem("w4_turned")
        w4_hi = sem("w4_hi")
        w4_split = sem("w4_split")
        to_abs = sem("to_abs")
        abs_ready = sem("abs_ready")
        xq_ready = sem("xq_ready")
        hq_ready = sem("hq_ready")
        hT_hi = sem("hT_hi")
        stored = sem("stored")

        block = ctx.enter_context(nc.Block())

        out_rows = out.rearrange("b (i p) d -> p (b i) d", p=P)

        W4_JOBS = [("gate", (0, 3)), ("gate", (3, 5)), ("up", (0, 3)), ("up", (3, 5)), ("tails", None),
                   ("down", 0), ("down", 1)]

        def w4_width(kind, part):
            return {"tails": D, "down": FF}.get(kind) or (part[1] - part[0]) * D

        def w4_loads(kind, part):
            if kind in ("gate", "up"):
                n0, n1 = part
                w = w_gate if kind == "gate" else w_up
                return [(q_x[:, 0:(n1 - n0) * D].rearrange("p (n k) -> p n k", k=D),
                         w[n0 * P:n1 * P, :].rearrange("(n p) k -> p n k", p=P))]
            if kind == "tails":
                return [(q_x[0:FTAIL, 0:D], w_gate[5 * P:FF, :]), (q_x[FTAIL:P, 0:D], w_up[5 * P:FF, :])]
            return [(q_x[:, 0:FF], w_down[part * P:(part + 1) * P, :])]

        def w4_loaded(n):
            return sum(2 if kind == "tails" else 1 for kind, _ in W4_JOBS[:n + 1])

        def w4_turns(kind, part, q):
            if kind in ("gate", "up"):
                n0, n1 = part
                m = 0 if kind == "gate" else FF
                return [([(q[:, (n - n0) * D + k * P:(n - n0) * D + (k + 1) * P], (n - n0) * P, P)
                          for n in range(n0, n1)],
                         [(P, 0, (n1 - n0) * P, lambda s, k=k: wgu[:, s, k, m + n0 * P:m + n1 * P])])
                        for k in range(KD)]
            if kind == "tails":
                return [([(q[:, k * P:(k + 1) * P], 0, P)],
                         [(P, m * FTAIL, FTAIL, lambda s, k=k, m=m: wgu[:, s, k, m * FF + 5 * P:(m + 1) * FF])
                          for m in range(2)]) for k in range(KD)]
            cols = slice(part * P, (part + 1) * P)
            return [([(q[:, c * P:c * P + (P if c < FK - 1 else FTAIL)], c % 3 * P, P if c < FK - 1 else FTAIL)
                      for c in range(3 * t, 3 * t + 3)],
                     [(P, c % 3 * P, P, lambda s, c=c: wdn[:, s, c, cols]) if c < FK - 1 else
                      (FTAIL, c % 3 * P, P, lambda s, c=c: wdn[0:FTAIL, s, c, cols])
                      for c in range(3 * t, 3 * t + 3)]) for t in range(2)]

        def w2_flat(part):
            return cut(opnd, W2 + part * 3 * 4 * 1024, 3 * 4 * 1024)

        def w3_flat(part):
            return cut(opnd, part * 8 * 1024, 8 * 1024)

        def x_half(t):
            return xn[:, 2 * t:2 * t + 2, :].rearrange("p a d -> p (a d)")

        def h_parts(part, t):
            for rows, c0, c1 in ((P, 0, 3),) if t == 0 else ((P, 3, 5), (FTAIL, 5, 6)):
                yield (hqT[0:rows, part, c0:c1, :],
                       bank[6 + t][0:rows, (c0 - 3 * t) * P:(c1 - 3 * t) * P].rearrange("p (c q) -> p c q", q=P))

        def tree_out(act, f, b):
            for o in range(KD if f < 2 else NBLK):
                act.wait_ge(*L2.filled(("tree", f, o), b))
                if f < 2:
                    act.activation((qT, kT)[f][:, 0, o, :], bank[o][:, :], ACT.Copy,
                                   scale=D ** -0.5 if f == 0 else 1.0).then_inc(tree_hi, 1)
                else:
                    act.activation(v2[:, 0, o, :], bank[o][:, 0:D], ACT.Copy).then_inc(tree_hi, 1)

        @block.sync
        def _(sp):
            sp.dma_start(idx[:, :], ids).then_inc(ids_in, 16)
            sp.dma_start(raw.rearrange("p a b -> p (a b)"), w1qkva).then_inc(w1_in, 16)
            sp.wait_ge(setup_done, 3)
            for dst, src in ((ident, ident_in), (gam1, gamma1), (nodew[:, :, 0:3 * NODES], node_w),
                             (nodeb, node_b.to_broadcast([P, 3 * NODES])), (bqs, bq), (bks, bk),
                             (asp, ascale_part), (asr, ascale_row.to_broadcast([P, HEADS])),
                             (bvs[64:128, :], bv)):
                sp.dma_start(dst, src).then_inc(consts_in, 16)
            for f in range(3):
                rows = TREE * f
                sp.dma_start(scan.rearrange("p a b -> p (a b)")[0:RT, :], route[f]).then_inc(route_in, 16)
                sp.wait_ge(route_in, 16 * (3 * f + 1))
                for r in range(2):
                    sp.dma_start(scan.rearrange("p a b -> p (a b)")[rows + LEAVES + r:rows + LEAVES + r + 1, :],
                                 b1[f:f + 1, :]).then_inc(route_in, 16)
                sp.wait_ge(route_split, f + 1)
                row = TREE * f + LEAVES + 1
                sp.dma_start(f32(route_w[row:row + 1, f, :]), f32(route_lo[row:row + 1, :])).then_inc(route_lo_moved, 16)
                sp.wait_ge(route_lo_moved, 16 * (f + 1))
            sp.dma_start(cut(data, A0, 3, D)[0:RT], b2).then_inc(consts_in, 16)
            sp.wait_ge(w1_ready, 2)
            with sp.Fori(0, NSEQ) as b:
                for k in range(6):
                    sp.wait_ge(raw_lo, b * 6 + k + 1)
                    sp.dma_start(raw[:, k % 3, :], w2raw[:, bass.ds(b * (6 * CH) + k * CH, CH)]
                                 ).then_inc(raw_in[k % 3], 16)
            for k in range(NCH3):
                if k < 4:
                    sp.wait_ge(*L2.emptied(("PV", 3), NSEQ - 1))
                    if k == 0:
                        sp.wait_ge(*L2.emptied(("PV", 2), NSEQ - 1))
                else:
                    sp.wait_ge(w3_prepared, k - 4 + 1)
                sp.dma_start(rawl[:, k % 4, :], w3raw[k]).then_inc(raw_in[k % 4], 16)
            for k, src in enumerate((bo, gamma3, beta3)):
                sp.dma_start(rows3[:, k, :], src.to_broadcast([P, D])).then_inc(rows3_in, 16)
            sp.wait_ge(h3_done, NSEQ)
            for n, (kind, part) in enumerate(W4_JOBS):
                if n:
                    sp.wait_ge(w4_quantized, n)
                for dst, src in w4_loads(kind, part):
                    sp.dma_start(dst, src).then_inc(w4_in, 16)
            with sp.Fori(0, NSEQ) as b:
                sp.wait_ge(*L4.emptied(("down", 2), b))
                sp.wait_ge(*L4.emptied(("down", 3), b))
                sp.dma_start(out_rows[:, bass.ds(b * NBLK, NBLK), :], h[:, bass.ds(b * NBLK, NBLK), :]
                             ).then_inc(stored, 16)
            sp.wait_ge(stored, 16 * NSEQ)

        @block.gpsimd
        def _(pool):
            pool.memset(neg_half, -0.5).then_inc(setup_done, 1)
            pool.memset(pos_half, 0.5).then_inc(setup_done, 1)
            pool.wait_ge(ids_in, 16)
            pool.wait_ge(setup_done, 3)

            def root(b, dst, src, exponent):
                return pool.tensor_tensor(dst, src, exponent, ALU.pow)

            for n in range(NSEQ * NBLK):
                pool.indirect_dma_start(h[:, n, :], None, table,
                                        bass.IndirectOffsetOnAxis(ap=idx[:, n:n + 1].bitcast(U32), axis=0)
                                        ).then_inc(rows_gathered, 16)
            with pool.Fori(0, NSEQ) as b:
                pool.wait_ge(var_ready, b + 1)
                root(b, sdev, mv[:, :, 1], pos_half)
                root(b, rstd, var_e, neg_half).then_inc(rstd_ready, 1)
                for k in range(6):
                    pool.wait_ge(raw_hi, b * 6 + k + 1)
                    at = bass.ds(b * 6 * CH + k * CH, CH)
                    pool.tensor_tensor(w2_flat(1)[:, at], raw[:, k % 3, :], f32(w2_flat(0)[:, at]),
                                       ALU.subtract).then_inc(raw_lo, 1)
            with pool.Fori(0, NSEQ) as b:
                pool.wait_ge(var_ready, b + (NSEQ + 1))
                root(b, rstd, var_e, neg_half).then_inc(rstd_ready, 1)
            with pool.Fori(0, NSEQ) as b:
                pool.wait_ge(var_ready, b * 2 + (2 * NSEQ + 1))
                root(b, rstd, var_e, neg_half).then_inc(rstd_ready, 1)
                for u in range(UNITS):
                    pool.wait_ge(rinv_ready, b * UNITS + u + 1)
                    if u >= 2:
                        pool.wait_ge(*L3.filled(("T", u - 2), b))
                    pool.sem_inc(pool_step, 1)
                    pool.tensor_scalar(pn3[:, u % 2, :], p3[:, u % 2, :], rinv[:, u % 4:u % 4 + 1], 1.0,
                                       ALU.mult, ALU.mult).then_inc(pn_ready, 1)
                pool.wait_ge(var_ready, b * 2 + (2 * NSEQ + 2))
                root(b, rstd, var_e, neg_half).then_inc(rstd_ready, 1)
            with pool.Fori(0, NSEQ) as b:
                pool.wait_ge(var_ready, b + (4 * NSEQ + 1))
                root(b, rstd, var_e, neg_half).then_inc(rstd_ready, 1)

        @block.tensor
        def _(pe):
            def product(dst, stat, mov, start, stop, **kw):
                pe.matmul(dst, stat(0), mov(0), start=start, stop=False, **kw)
                pe.matmul(dst, stat(0), mov(1), start=False, stop=False, **kw)
                return pe.matmul(dst, stat(1), mov(0), start=False, stop=stop, **kw)

            def turn_x(L, b, ready, base, per=NBLK):
                for k in range(KD):
                    pe.wait_ge(*L.room(("xT", k), b))
                for i in range(NBLK):
                    if i % (NBLK // per) == 0:
                        pe.wait_ge(ready, b * per + (base + i // (NBLK // per) + 1))
                    for k in range(KD):
                        mm = pe.transpose(bank[L.place[("xT", k)][0]][:, i * P:(i + 1) * P],
                                          xn[:, i, k * P:(k + 1) * P], ident)
                        if i == NBLK - 1:
                            mm.then_inc(L.fill(("xT", k)), 1)

            pe.wait_ge(consts_in, 16 * 10)
            pe.wait_ge(w1_ready, 2)
            with pe.Fori(0, NSEQ) as b:
                turn_x(L1, b, xn_ready, 0)
                for k in range(KD):
                    pe.wait_ge(*L1.emptied(("xT", k), b))
                for c in range(KD):
                    for what, e in (("a", 2 * KD + c), ("kv", KD + c), ("q", c)):
                        pe.wait_ge(*L1.room((what, c), b))
                        dst = bank[L1.place[(what, c)][0]]
                        for k in range(KD):
                            mm = product(dst[:, :], lambda s: w1[:, s, k, e * P:(e + 1) * P],
                                         lambda s: xT[:, s, k, :], k == 0, k == KD - 1)
                        mm.then_inc(L1.fill((what, c)), 1)
                for t in range(2):
                    pe.wait_ge(*L1.room(("back", t), b))
                for c in range(KD):
                    pe.wait_ge(*L1.emptied(("q", c), b))
                    for i in range(NBLK):
                        mm = pe.transpose(bank[i // 2][:, i % 2 * D + c * P:i % 2 * D + (c + 1) * P],
                                          scan[:, c, i * P:(i + 1) * P], ident)
                        if c == KD - 1 and i % 2:
                            mm.then_inc(L1.fill(("back", i // 2)), 1)
            pe.wait_ge(raw_lo, 3 + NCH2)
            pe.wait_ge(route_lo_moved, 48)
            with pe.Fori(0, NSEQ) as b:
                turn_x(L2, b, xn_ready, NSEQ * NBLK)
                for k in range(KD):
                    pe.wait_ge(*L2.emptied(("xT", k), b))
                pe.wait_ge(*L2.room("node", b))
                for i in range(NBLK):
                    for k in range(KD):
                        mm = product(bank[2][:, i * 64:i * 64 + NNODE], lambda s: xT[:, s, k, i * P:(i + 1) * P],
                                     lambda s: noder[:, s, k, :], k == 0, k == KD - 1)
                mm.then_inc(L2.fill("node"), 1)

                def w1_block(f, j):
                    what = ("hid", f, j)
                    pe.wait_ge(*L2.room(what, b))
                    dst = bank[hid_bank[f, j]][:, :]
                    cols = slice(j * P, (j + 1) * P)
                    for k in range(KD):
                        product(dst, lambda s: w2[:, s, f, k, cols], lambda s: xT[:, s, k, :], k == 0, False)
                    if (f, j) == (0, 0):
                        route_rows()
                    pe.matmul(dst, route_w[0:RT, f, cols], selT[0:RT, 0, :], start=False, stop=True
                              ).then_inc(L2.fill(what), 1)

                def route_rows():
                    pe.wait_ge(*L2.room("selT", b))
                    pe.wait_ge(*L2.room("takT", b))
                    pe.wait_ge(sel_ready, b + 1)
                    for s, what in ((0, "selT"), (1, "takT")):
                        for i in range(NBLK):
                            mm = pe.transpose(bank[3 + s][0:RT, i * P:(i + 1) * P], sel[:, i, s, :], ident)
                        mm.then_inc(L2.fill(what), 1)
                    pe.wait_ge(*L2.emptied("selT", b))
                    pe.wait_ge(*L2.emptied("takT", b))

                def w2_block(f, j):
                    slot = (NH2 * f + j) % 3
                    pe.wait_ge(*L2.emptied(("hid", f, j), b))
                    w2j = lambda s: w2[:, s, f, 2 + j // 4, j % 4 * D:(j % 4 + 1) * D]
                    for o in range(KD if f < 2 else NBLK):
                        cols = slice(o * P, (o + 1) * P)
                        if j == 0:
                            pe.wait_ge(*L2.room(("tree", f, o), b))
                        if f < 2:
                            dst = bank[o][:, :]
                            if j == 0:
                                pe.matmul(dst, b2w[0:RT, 0, f, cols], selT[0:RT, 1, :], start=True, stop=False)
                                pe.matmul(dst, b2w[0:RT, 1, f, cols], selT[0:RT, 1, :], start=False, stop=False)
                            mm = product(dst, lambda s: w2j(s)[:, cols], lambda s: hid[:, slot, s, :],
                                         False, j == NH2 - 1)
                        else:
                            dst = bank[o][:, 0:D]
                            if j == 0:
                                pe.matmul(dst, selT[0:RT, 1, cols], b2w[0:RT, 0, f, :], start=True, stop=False)
                                pe.matmul(dst, selT[0:RT, 1, cols], b2w[0:RT, 1, f, :], start=False, stop=False)
                            mm = product(dst, lambda s: hid[:, slot, s, cols], w2j, False, j == NH2 - 1)
                        if j == NH2 - 1:
                            mm.then_inc(L2.fill(("tree", f, o)), 1)

                seq = [(f, j) for f in range(3) for j in range(NH2)]
                for n in range(len(seq) + 2):
                    if n < len(seq):
                        w1_block(*seq[n])
                    if n >= 2:
                        w2_block(*seq[n - 2])

                def scores(i):
                    pe.wait_ge(*L2.room(("S", i), b))
                    if i == 0:
                        for f in range(2):
                            for o in range(KD):
                                pe.wait_ge(*L2.emptied(("tree", f, o), b))
                    for k in range(KD):
                        mm = product(bank[4 + i % 2][:, :], lambda s: qT[:, s, k, i * P:(i + 1) * P],
                                     lambda s: kT[:, s, k, :], k == 0, k == KD - 1)
                    mm.then_inc(L2.fill(("S", i)), 1)

                def turn_p(i):
                    pe.wait_ge(*L2.room(("T", i), b))
                    pe.wait_ge(*L2.emptied(("S", i), b))
                    for kb in range(NBLK):
                        mm = pe.transpose(bank[6 + i % 2][:, kb * P:(kb + 1) * P], p2[:, i % 2, kb * P:(kb + 1) * P],
                                          ident)
                    mm.then_inc(L2.fill(("T", i)), 1)

                def weigh(i):
                    pe.wait_ge(*L2.room(("PV", i), b))
                    if i == 0:
                        for o in range(NBLK):
                            pe.wait_ge(*L2.emptied(("tree", 2, o), b))
                    pe.wait_ge(*L2.emptied(("T", i), b))
                    for kb in range(NBLK):
                        mm = product(bank[i % 2][:, 0:D], lambda s: pT2[:, i % 2, s, kb * P:(kb + 1) * P],
                                     lambda s: v2[:, s, kb, :], kb == 0, kb == NBLK - 1)
                    mm.then_inc(L2.fill(("PV", i)), 1)

                scores(0)
                scores(1)
                for i in range(NBLK):
                    turn_p(i)
                    if i + 2 < NBLK:
                        scores(i + 2)
                    weigh(i)
            pe.wait_ge(w3_prepared, NCH3)
            with pe.Fori(0, NSEQ) as b:
                turn_x(L3, b, xn_ready, 2 * NSEQ * NBLK)
                for k in range(KD):
                    pe.wait_ge(*L3.emptied(("xT", k), b))
                for s_ in STEPS3:
                    what = s_[0]
                    if what in ("Q", "K"):
                        pair = s_[1]
                        pe.wait_ge(*L3.room(s_, b))
                        m = 2 * (what == "K")
                        for k in range(KD):
                            mm = product(bank[5][:, :], lambda s: w3[:, s, m + k, pair * P:(pair + 1) * P],
                                         lambda s: xT[:, s, k, :], k == 0, k == KD - 1)
                        mm.then_inc(L3.fill(s_), 1)
                    elif what == "V":
                        _, quarter, t = s_
                        pe.wait_ge(*L3.room(s_, b))
                        for kb in (2 * t, 2 * t + 1):
                            for k in range(KD):
                                mm = product(bank[5][:, kb % 2 * D:kb % 2 * D + D],
                                             lambda s: xT[:, s, k, kb * P:(kb + 1) * P],
                                             lambda s: w3[:, s, 4 + k, quarter * D:(quarter + 1) * D],
                                             k == 0, k == KD - 1)
                        mm.then_inc(L3.fill(s_), 1)
                    elif what == "S":
                        u = s_[1]
                        head, i = divmod(u, NBLK)
                        pair, rows = head // 2, slice(head % 2 * HDIM, head % 2 * HDIM + HDIM)
                        if u % (2 * NBLK) == 0:
                            pe.wait_ge(*L3.emptied(("Q", pair), b))
                            pe.wait_ge(*L3.emptied(("K", pair), b))
                        pe.wait_ge(*L3.room(s_, b))
                        product(bank[u % 2][:, :], lambda s: qk[rows, pair % 2, 0, s, i * P:(i + 1) * P],
                                lambda s: qk[rows, pair % 2, 1, s, :], True, True).then_inc(L3.fill(s_), 1)
                    elif what == "T":
                        u = s_[1]
                        pe.wait_ge(*L3.room(s_, b))
                        pe.wait_ge(pn_ready, b * UNITS + u + 1)
                        for kb in range(NBLK):
                            mm = pe.transpose(bank[2 + u % 2][:, kb * P:(kb + 1) * P],
                                              pn3[:, u % 2, kb * P:(kb + 1) * P], ident)
                        mm.then_inc(L3.fill(s_), 1)
                    elif what == "PV":
                        head, half = divmod(s_[1], 2)
                        if half == 0:
                            pe.wait_ge(*L3.room(("PV", head), b))
                        if head % 4 == 0 and half == 0:
                            for t in range(2):
                                pe.wait_ge(*L3.emptied(("V", head // 4, t), b))
                        pe.wait_ge(*L3.emptied(("T", 2 * s_[1]), b))
                        pe.wait_ge(*L3.emptied(("T", 2 * s_[1] + 1), b))
                        for kb in range(NBLK):
                            for s in range(SPLIT):
                                mm = pe.matmul(bank[4][:, half * D:(half + 1) * D],
                                               vs[:, head // 4 % 2, kb, head % 4, :], pT3[:, half, s, kb, :],
                                               start=(kb == 0 and s == 0), stop=(kb == NBLK - 1 and s == 1))
                        if half == 1:
                            mm.then_inc(L3.fill(("PV", head)), 1)
                    elif what == "O":
                        pair = s_[1]
                        if pair == 0:
                            for t in range(2):
                                pe.wait_ge(*L3.room(("O", t), b))
                        pe.wait_ge(at_ready, b * PAIRS + pair + 1)
                        for i in range(NBLK):
                            mm = product(bank[6 + i // 2][:, i % 2 * D:(i % 2 + 1) * D],
                                         lambda s: at3[pair % 2][:, s, i * P:(i + 1) * P],
                                         lambda s: w3[:, s, 6 + pair // 4, pair % 4 * D:(pair % 4 + 1) * D],
                                         pair == 0 and i % 2 == 0, pair == PAIRS - 1, skip_group_check=True)
                            if pair == PAIRS - 1 and i % 2:
                                mm.then_inc(L3.fill(("O", i // 2)), 1)
            n_banks = 0
            for n, (kind, part) in enumerate(W4_JOBS):
                pe.wait_ge(w4_quantized, n + 1)
                for turns, _ in w4_turns(kind, part, q_c[:, 0, :]):
                    if n_banks >= 2:
                        pe.wait_ge(w4_split, n_banks - 1)
                    for src, at, rows in turns:
                        mm = pe.transpose(bank[n_banks % 2][0:rows, at:at + P], src, ident)
                    mm.then_inc(w4_turned, 1)
                    n_banks += 1
            pe.wait_ge(w4_split, n_banks)
            with pe.Fori(0, NSEQ) as b:
                turn_x(L4, b, xq_ready, 0, 2)
                for k in range(KD):
                    pe.wait_ge(*L4.emptied(("xT", k), b))

                def gate_up(i):
                    for m, what in enumerate(("gate", "up")):
                        for t in range(2):
                            pe.wait_ge(*L4.room((what, i, t), b))
                            lo = m * FF + t * (FF // 2)
                            for k in range(KD):
                                mm = product(bank[2 + 2 * m + t][:, 0:FF // 2],
                                             lambda s: xT[:, s, k, i * P:(i + 1) * P],
                                             lambda s: wgu[:, s, k, lo:lo + FF // 2], k == 0, k == KD - 1)
                            mm.then_inc(L4.fill((what, i, t)), 1)

                def turn_h(i):
                    pe.wait_ge(hq_ready, b * NBLK + i + 1)
                    for t in range(2):
                        pe.wait_ge(*L4.room(("hT", i, t), b))
                        for c in range(3 * t, 3 * t + 3):
                            rows = P if c < FK - 1 else FTAIL
                            mm = pe.transpose(bank[6 + t][0:rows, c % 3 * P:c % 3 * P + P],
                                              q_c[:, i % 2, c * P:c * P + rows], ident)
                        mm.then_inc(L4.fill(("hT", i, t)), 1)

                def down(i):
                    pe.wait_ge(*L4.room(("down", i), b))
                    for t in range(2):
                        pe.wait_ge(*L4.emptied(("hT", i, t), b))
                    for c in range(FK):
                        rows = P if c < FK - 1 else FTAIL
                        mm = product(bank[i % 2][:, 0:D], lambda s: hqT[0:rows, s, c, :],
                                     lambda s: wdn[0:rows, s, c, :], c == 0, c == FK - 1)
                    mm.then_inc(L4.fill(("down", i)), 1)

                gate_up(0)
                for i in range(NBLK):
                    if i + 1 < NBLK:
                        gate_up(i + 1)
                    turn_h(i)
                    down(i)

        @block.scalar
        def _(act):
            def x_hi(L, b, base, scale=None):
                for k in range(KD):
                    act.wait_ge(*L.filled(("xT", k), b))
                    src = bank[L.place[("xT", k)][0]][:, :]
                    if scale is None:
                        ins = act.activation(xT[:, 0, k, :], src, ACT.Copy)
                    else:
                        ins = act.activation(xT[:, 0, k, :], src, ACT.Identity, scale=scale[:, k:k + 1])
                    ins.then_inc(xhi_ready, 1)

            act.wait_ge(w1_in, 16)
            act.activation(w1[:, 0, :, :].rearrange("p a b -> p (a b)"), raw.rearrange("p a b -> p (a b)"),
                           ACT.Copy).then_inc(w1_ready, 1)
            act.wait_ge(consts_in, 16 * 10)
            with act.Fori(0, NSEQ) as b:
                x_hi(L1, b, 0, gam1)
                for c in range(KD):
                    act.wait_ge(*L1.filled(("a", c), b))
                    act.activation(gate[:, c, :], bank[L1.place[("a", c)][0]][:, :], ACT.Sigmoid
                                   ).then_inc(L1.empty(("a", c)), 1)
                for k in range(6):
                    act.wait_ge(raw_in[k % 3], b * 32 + 16 * (k // 3 + 1))
                    act.activation(w2_flat(0)[:, bass.ds(b * 6 * CH + k * CH, CH)], raw[:, k % 3, :], ACT.Copy
                                   ).then_inc(raw_hi, 1)
            with act.Fori(0, NSEQ) as b:
                x_hi(L2, b, NSEQ * KD)
                for s, what in ((0, "selT"), (1, "takT")):
                    act.wait_ge(*L2.filled(what, b))
                    act.activation(selT[0:RT, s, :], bank[3 + s][0:RT, :], ACT.Copy).then_inc(L2.empty(what), 1)
                for f in range(3):
                    for j in range(NH2):
                        n = NH2 * f + j
                        act.wait_ge(*L2.filled(("hid", f, j), b))
                        act.activation(hid[:, n % 3, 0, :], bank[hid_bank[f, j]][:, :], ACT.Relu
                                       ).then_inc(hid_hi, 1)
                        if f and j == 1:
                            tree_out(act, f - 1, b)
                tree_out(act, 2, b)

                def exps(i):
                    act.wait_ge(nmax_ready, b * NBLK + i + 1)
                    act.activation(p2[:, i % 2, :], bank[4 + i % 2][:, :], ACT.Exp, bias=nmax[:, i:i + 1],
                                   accum_out=rsum[:, i:i + 1]).then_inc(L2.empty(("S", i)), 1)

                exps(0)
                exps(1)
                for i in range(NBLK):
                    act.wait_ge(*L2.filled(("T", i), b))
                    act.activation(pT2[:, i % 2, 0, :], bank[6 + i % 2][:, :], ACT.Copy).then_inc(p_hi, 1)
                    if i + 2 < NBLK:
                        exps(i + 2)
            for k in range(NCH3):
                if k < 4:
                    act.wait_ge(w3_prepared_q, k + 1)
                else:
                    act.wait_ge(raw_in[k % 4], (0 if k % 4 == 3 else 16 * 2 * NSEQ) + 16 * (k // 4 + 1))
                act.activation(w3_flat(0)[:, k * CH:(k + 1) * CH], rawl[:, k % 4, :], ACT.Copy
                               ).then_inc(w3_hi, 1)
            with act.Fori(0, NSEQ) as b:
                x_hi(L3, b, 2 * NSEQ * KD)
                for s_ in STEPS3:
                    what = s_[0]
                    if what in ("Q", "K"):
                        pair, m = s_[1], int(what == "K")
                        act.wait_ge(*L3.filled(s_, b))
                        act.activation(qk[:, pair % 2, m, 0, :], bank[5][:, :], ACT.Identity,
                                       bias=(bks if m else bqs)[:, pair:pair + 1]).then_inc(proj_hi, 1)
                    elif what == "V":
                        _, quarter, t = s_
                        act.wait_ge(*L3.filled(s_, b))
                        act.activation(vs[:, quarter % 2, 2 * t:2 * t + 2, :, 0:HDIM],
                                       bank[5][:, :].rearrange("p (a g d) -> p a g d", a=2, g=4), ACT.Copy
                                       ).then_inc(proj_hi, 1)
                    elif what == "S":
                        u = s_[1]
                        act.wait_ge(nmax_ready, b * UNITS + (NSEQ * NBLK + u + 1))
                        if u >= 2:
                            act.wait_ge(pn_ready, b * UNITS + (u - 1))
                        act.activation(p3[:, u % 2, :], bank[u % 2][:, :], ACT.Exp, bias=nmax[:, u % 4:u % 4 + 1],
                                       accum_out=rsum[:, u % 4:u % 4 + 1]).then_inc(L3.empty(s_), 1)
                    elif what == "T":
                        u = s_[1]
                        act.wait_ge(*L3.filled(s_, b))
                        act.activation(pT3[:, u // 2 % 2, 0, :, u % 2 * P:(u % 2 + 1) * P],
                                       bank[2 + u % 2][:, :].rearrange("p (k q) -> p k q", k=NBLK), ACT.Copy
                                       ).then_inc(p_hi, 1)
                    elif what == "PV" and s_[1] % 2:
                        head = s_[1] // 2
                        act.wait_ge(*L3.filled(("PV", head), b))
                        act.activation(att_lo[0:HDIM, :], bank[4][HDIM:P, :], ACT.Identity,
                                       bias=bvs[HDIM:P, head:head + 1]).then_inc(att_shift, 1)
                        if head % 2:
                            act.wait_ge(*L3.emptied(("PV", head), b))
                            act.activation(at3[head // 2 % 2][:, 0, :], att, ACT.Copy).then_inc(att_hi, 1)
            n_banks = 0
            for n, (kind, part) in enumerate(W4_JOBS):
                act.wait_ge(w4_in, 16 * w4_loaded(n))
                if n:
                    act.wait_ge(w4_quantized, n)
                w = w4_width(kind, part)
                act.activation(q_a[:, 0:w], q_x[:, 0:w], ACT.Abs).then_inc(w4_abs, 1)
                for _, parts in w4_turns(kind, part, q_c[:, 0, :]):
                    act.wait_ge(w4_turned, n_banks + 1)
                    for rows, at, cols, dst in parts:
                        ins = act.activation(dst(0), bank[n_banks % 2][0:rows, at:at + cols], ACT.Copy)
                    ins.then_inc(w4_hi, 1)
                    n_banks += 1
            with act.Fori(0, NSEQ) as b:
                def magnitude(src):
                    act.activation(q_a[:, 0:src.shape[1]], src, ACT.Abs).then_inc(abs_ready, 1)

                act.wait_ge(to_abs, b + 1)
                magnitude(x_half(0))
                act.wait_ge(xq_ready, b * 2 + 1)
                magnitude(x_half(1))
                x_hi(L4, b, 3 * NSEQ * KD)
                for i in range(NBLK):
                    for t in range(2):
                        act.wait_ge(*L4.filled(("gate", i, t), b))
                        act.activation(silu[:, t * (FF // 2):(t + 1) * (FF // 2)], bank[2 + t][:, 0:FF // 2],
                                       ACT.Silu).then_inc(L4.empty(("gate", i, t)), 1)
                    act.wait_ge(*L4.emptied(("up", i, 1), b))
                    magnitude(q_x[:, 0:FF])
                    for t in range(2):
                        act.wait_ge(*L4.filled(("hT", i, t), b))
                        for dst, src in h_parts(0, t):
                            ins = act.activation(dst, src, ACT.Copy)
                        ins.then_inc(hT_hi, 1)

        @block.vector
        def _(dve):
            steps = Steps(dve_step)

            def link(ins):
                steps.link(dve, ins)

            for k in range(8):
                dve.sem_inc(banks.emptied_sem[k], 1)
            dve.sem_inc(raw_lo, 3)

            def moments(src):
                for i in range(NBLK):
                    ins = dve.bn_stats(stats[:, i, :], src(i))
                link(ins)
                dve.memset(var_e, 0.0)
                for i in range(NBLK):
                    ins = dve.bn_aggr(mv[:, i, :], stats[:, i, :])
                link(ins)
                dve.tensor_scalar(var_e, mv[:, :, 1], LN_EPS, None, ALU.add).then_inc(var_ready, 1)

            def h_at(b, i, n=1):
                ap = h[:, bass.ds(b * NBLK + i, n), :]
                return ap.rearrange("p a d -> p (a d)")

            def normalize(b, mult, done):
                for i in range(NBLK):
                    dve.tensor_scalar(xn[:, i, :], h_at(b, i), mv[:, i, 0:1], mult[:, i:i + 1],
                                      ALU.subtract, ALU.mult).then_inc(done, 1)

            def x_lo(L, b, base, scale=None):
                for k in range(KD):
                    dve.wait_ge(*L.filled(("xT", k), b))
                    dve.wait_ge(xhi_ready, b * KD + (base + k + 1))
                    src = bank[L.place[("xT", k)][0]][:, :]
                    if scale is None:
                        ins = dve.tensor_tensor(xT[:, 1, k, :], src, f32(xT[:, 0, k, :]), ALU.subtract)
                    else:
                        ins = dve.scalar_tensor_tensor(xT[:, 1, k, :], src, scale[:, k:k + 1],
                                                       f32(xT[:, 0, k, :]), ALU.mult, ALU.subtract)
                    ins.then_inc(L.empty(("xT", k)), 1)

            steps.start(0, 4)
            dve.memset(nodew, 0.0).then_inc(setup_done, 1)
            dve.wait_ge(w1_in, 16)
            dve.wait_ge(w1_ready, 1)
            dve.tensor_tensor(w1[:, 1, :, :].rearrange("p a b -> p (a b)"), raw.rearrange("p a b -> p (a b)"),
                              f32(w1[:, 0, :, :].rearrange("p a b -> p (a b)")), ALU.subtract).then_inc(w1_ready, 1)
            for f in range(3):
                dve.wait_ge(route_in, 16 * 3 * (f + 1))
                src = scan.rearrange("p a b -> p (a b)")[0:RT, :]
                link(dve.tensor_copy(route_w[0:RT, f, :], src))
                if f:
                    dve.wait_ge(route_lo_moved, 16 * f)
                dve.tensor_tensor(route_lo[0:RT, :], src, f32(route_w[0:RT, f, :]), ALU.subtract
                                  ).then_inc(route_split, 1)
            dve.wait_ge(consts_in, 16 * 10)
            b2s = cut(data, A0, 3, D)[0:RT]
            dve.tensor_copy(noder[:, 0, :, :], nodew)
            link(dve.tensor_copy(b2w[0:RT, 0, :, :], b2s))
            dve.tensor_tensor(noder[:, 1, :, :], nodew, f32(noder[:, 0, :, :]), ALU.subtract)
            dve.tensor_tensor(b2w[0:RT, 1, :, :], b2s, f32(b2w[0:RT, 0, :, :]), ALU.subtract)
            steps.end()
            dve.wait_ge(rows_gathered, 16 * NSEQ * NBLK)
            with dve.Fori(0, NSEQ) as b:
                steps.start(b, 5)
                moments(lambda i: h_at(b, i))
                dve.wait_ge(rstd_ready, b + 1)
                link(dve.scalar_tensor_tensor(coef, sdev, D ** 0.5, rstd, ALU.mult, ALU.mult))
                link(dve.tensor_scalar(coef, coef, 1e-12, None, ALU.max))
                link(dve.reciprocal(coef, coef))
                dve.scalar_tensor_tensor(coef, coef, D ** 0.5, rstd, ALU.mult, ALU.mult).then_inc(coef_ready, 1)
                dve.wait_ge(coef_ready, b + 1)
                normalize(b, coef, xn_ready)
                x_lo(L1, b, 0, gam1)
                for c in range(KD):
                    dve.wait_ge(*L1.filled(("kv", c), b))
                    dve.wait_ge(*L1.emptied(("a", c), b))
                    dve.tensor_tensor_scan(scan[:, c, :], gate[:, c, :], bank[L1.place[("kv", c)][0]][:, :], 0.0,
                                           ALU.mult, ALU.add).then_inc(L1.empty(("kv", c)), 1)
                    dve.wait_ge(*L1.filled(("q", c), b))
                    dve.wait_ge(*L1.emptied(("kv", c), b))
                    dve.tensor_tensor(scan[:, c, :], bank[L1.place[("q", c)][0]][:, :], scan[:, c, :], ALU.mult
                                      ).then_inc(L1.empty(("q", c)), 1)
                for t in range(2):
                    dve.wait_ge(*L1.filled(("back", t), b))
                    dve.tensor_tensor(h_at(b, 2 * t, 2), bank[t][:, :], h_at(b, 2 * t, 2), ALU.add
                                      ).then_inc(L1.empty(("back", t)), 1)
                steps.end()
            for t in range(2):
                dve.wait_ge(*L1.emptied(("back", t), NSEQ - 1))
            steps.start(0, 2)
            link(dve.memset(sel.rearrange("p a b c -> p (a b c)"), 0.0))
            for f in range(3):
                ins = dve.memset(sel[:, :, 0, TREE * f + LEAVES:TREE * f + LEAVES + 2], 1.0)
            link(ins)
            steps.end()
            with dve.Fori(0, NSEQ) as b:
                steps.start(b, 11)
                moments(lambda i: h_at(b, i))
                dve.wait_ge(rstd_ready, b + (NSEQ + 1))
                normalize(b, rstd, xn_ready)
                x_lo(L2, b, NSEQ * KD)
                dve.wait_ge(*L2.filled("node", b))
                dve.tensor_tensor(score, bank[2][:, 0:NBLK * 64].rearrange("p (i n) -> p i n", n=64)[:, :, 0:3 * NODES],
                                  nodeb.rearrange("p (a n) -> p a n", a=1).to_broadcast([P, NBLK, 3 * NODES]),
                                  ALU.add).then_inc(L2.empty("node"), 1)
                dve.wait_ge(*L2.emptied("node", b))
                link(dve.tensor_scalar(score, score, 0.0, None, ALU.is_ge))
                g = score.rearrange("p i (f n) -> p i f n", f=3)
                for level in range(DEPTH):
                    n = 2 ** level
                    gl = g[:, :, :, n - 1:2 * n - 1]
                    if level < DEPTH - 1:
                        kids = path[:, level, :, :, 0:2 * n].rearrange("p i f (n c) -> p i f n c", c=2)
                        left, right = kids[:, :, :, :, 0], kids[:, :, :, :, 1]
                    else:
                        kids = sel[:, :, 1, :].rearrange("p i (f n) -> p i f n", f=3)[:, :, :, 0:LEAVES].rearrange(
                            "p i f (n c) -> p i f n c", c=2)
                        left, right = kids[:, :, :, :, 0], kids[:, :, :, :, 1]
                    if level == 0:
                        dve.tensor_scalar(left, gl, -1.0, 1.0, ALU.mult, ALU.add)
                        link(dve.tensor_copy(right, gl))
                    else:
                        up = path[:, level - 1, :, :, 0:n]
                        link(dve.tensor_tensor(right, up, gl, ALU.mult))
                        link(dve.tensor_tensor(left, up, right, ALU.subtract))
                dve.tensor_scalar(sel[:, :, 0, :].rearrange("p i (f n) -> p i f n", f=3)[:, :, :, 0:LEAVES],
                                  sel[:, :, 1, :].rearrange("p i (f n) -> p i f n", f=3)[:, :, :, 0:LEAVES],
                                  -1.0, None, ALU.add).then_inc(sel_ready, 1)

                def tree_lo(f):
                    for o in range(KD if f < 2 else NBLK):
                        n = KD * f + o
                        dve.wait_ge(*L2.filled(("tree", f, o), b))
                        dve.wait_ge(tree_hi, b * (2 * KD + NBLK) + n + 1)
                        if f == 0:
                            ins = dve.scalar_tensor_tensor(qT[:, 1, o, :], bank[o][:, :], D ** -0.5,
                                                           f32(qT[:, 0, o, :]), ALU.mult, ALU.subtract)
                        elif f == 1:
                            ins = dve.tensor_tensor(kT[:, 1, o, :], bank[o][:, :], f32(kT[:, 0, o, :]), ALU.subtract)
                        else:
                            ins = dve.tensor_tensor(v2[:, 1, o, :], bank[o][:, 0:D], f32(v2[:, 0, o, :]),
                                                    ALU.subtract)
                        ins.then_inc(L2.empty(("tree", f, o)), 1)

                for f in range(3):
                    for j in range(NH2):
                        n = NH2 * f + j
                        dve.wait_ge(*L2.filled(("hid", f, j), b))
                        dve.wait_ge(hid_hi, b * (3 * NH2) + n + 1)
                        dve.scalar_tensor_tensor(hid[:, n % 3, 1, :], bank[hid_bank[f, j]][:, :], 0.0,
                                                 f32(hid[:, n % 3, 0, :]), ALU.max, ALU.subtract
                                                 ).then_inc(L2.empty(("hid", f, j)), 1)
                        if f and j == 1:
                            tree_lo(f - 1)
                tree_lo(2)

                def row_max(i):
                    dve.wait_ge(*L2.filled(("S", i), b))
                    dve.tensor_reduce(nmax[:, i:i + 1], bank[4 + i % 2][:, :], AX.X, ALU.max, negate=True
                                      ).then_inc(nmax_ready, 1)

                def add_out(i):
                    dve.wait_ge(*L2.filled(("PV", i), b))
                    dve.scalar_tensor_tensor(h_at(b, i), bank[i % 2][:, 0:D], rinv[:, i:i + 1], h_at(b, i),
                                             ALU.mult, ALU.add).then_inc(L2.empty(("PV", i)), 1)

                row_max(0)
                row_max(1)
                for i in range(NBLK):
                    dve.wait_ge(*L2.emptied(("S", i), b))
                    ins = dve.reciprocal(rinv[:, i:i + 1], rsum[:, i:i + 1])
                    if i == NBLK - 1:
                        link(ins)
                    dve.wait_ge(*L2.filled(("T", i), b))
                    dve.wait_ge(p_hi, b * NBLK + i + 1)
                    dve.tensor_tensor(pT2[:, i % 2, 1, :], bank[6 + i % 2][:, :], f32(pT2[:, i % 2, 0, :]),
                                      ALU.subtract).then_inc(L2.empty(("T", i)), 1)
                    if i + 2 < NBLK:
                        row_max(i + 2)
                    if i:
                        dve.wait_ge(*L2.emptied(("T", i), b))
                        add_out(i - 1)
                add_out(NBLK - 1)
                steps.end()
            for i in (2, 3):
                dve.wait_ge(*L2.emptied(("PV", i), NSEQ - 1))
            steps.start(0, 2)
            dve.tensor_scalar(asr, asr, HDIM ** -0.5, None, ALU.mult)
            link(dve.tensor_scalar(asp, asp, HDIM ** -0.5, None, ALU.mult))
            link(dve.tensor_tensor(bqs, bqs, asp, ALU.mult))
            steps.end()
            for k in range(4):
                dve.wait_ge(raw_in[k % 4], (0 if k % 4 == 3 else 16 * 2 * NSEQ) + 16)
                heads = slice((k % 2) * CH // HDIM, (k % 2 + 1) * CH // HDIM)
                piece = rawl[:, k, :].rearrange("p (g d) -> p g d", d=HDIM)
                dve.tensor_tensor(piece, piece, asr[:, heads].rearrange("p (g a) -> p g a", a=1).to_broadcast(
                    [P, CH // HDIM, HDIM]), ALU.mult).then_inc(w3_prepared_q, 1)
            for k in range(NCH3):
                dve.wait_ge(w3_hi, k + 1)
                dve.wait_ge(raw_in[k % 4], (0 if k % 4 == 3 else 16 * 2 * NSEQ) + 16 * (k // 4 + 1))
                if k == 0:
                    dve.wait_ge(w3_prepared_q, 4)
                dve.tensor_tensor(w3_flat(1)[:, k * CH:(k + 1) * CH], rawl[:, k % 4, :],
                                  f32(w3_flat(0)[:, k * CH:(k + 1) * CH]), ALU.subtract).then_inc(w3_prepared, 1)
            dve.wait_ge(w3_prepared, NCH3)
            dve.wait_ge(rows3_in, 48)
            with dve.Fori(0, NSEQ) as b:
                steps.start(b, 2 + 1 + 2 + 3)
                moments(lambda i: h_at(b, i))
                dve.wait_ge(rstd_ready, b * 2 + (2 * NSEQ + 1))
                normalize(b, rstd, xn_ready)
                x_lo(L3, b, 2 * NSEQ * KD)
                nproj = 0
                PROJ = 2 * PAIRS + 2 * QUARTERS
                for s_ in STEPS3:
                    what = s_[0]
                    if what in ("Q", "K"):
                        pair, m = s_[1], int(what == "K")
                        nproj += 1
                        dve.wait_ge(*L3.filled(s_, b))
                        dve.wait_ge(proj_hi, b * PROJ + nproj)
                        dve.scalar_tensor_tensor(qk[:, pair % 2, m, 1, :], bank[5][:, :],
                                                 (bks if m else bqs)[:, pair:pair + 1], f32(qk[:, pair % 2, m, 0, :]),
                                                 ALU.add, ALU.subtract).then_inc(L3.empty(s_), 1)
                    elif what == "V":
                        _, quarter, t = s_
                        nproj += 1
                        dve.wait_ge(*L3.filled(s_, b))
                        dve.wait_ge(proj_hi, b * PROJ + nproj)
                        dst = vs[:, quarter % 2, 2 * t:2 * t + 2, :, :]
                        src = bank[5][:, :].rearrange("p (a g d) -> p a g d", a=2, g=4)
                        dve.tensor_tensor(dst[:, :, :, HDIM:P], src, f32(dst[:, :, :, 0:HDIM]), ALU.subtract
                                          ).then_inc(L3.empty(s_), 1)
                    elif what == "S":
                        u = s_[1]
                        dve.wait_ge(*L3.filled(s_, b))
                        dve.tensor_reduce(nmax[:, u % 4:u % 4 + 1], bank[u % 2][:, :], AX.X, ALU.max, negate=True
                                          ).then_inc(nmax_ready, 1)
                        dve.wait_ge(*L3.emptied(s_, b))
                        dve.reciprocal(rinv[:, u % 4:u % 4 + 1], rsum[:, u % 4:u % 4 + 1]).then_inc(rinv_ready, 1)
                    elif what == "T":
                        u = s_[1]
                        dve.wait_ge(*L3.filled(s_, b))
                        dve.wait_ge(p_hi, b * UNITS + (NSEQ * NBLK + u + 1))
                        half = pT3[:, u // 2 % 2, :, :, u % 2 * P:(u % 2 + 1) * P]
                        dve.tensor_tensor(half[:, 1], bank[2 + u % 2][:, :].rearrange("p (k q) -> p k q", k=NBLK),
                                          f32(half[:, 0]), ALU.subtract).then_inc(L3.empty(s_), 1)
                    elif what == "PV" and s_[1] % 2:
                        head = s_[1] // 2
                        dve.wait_ge(att_shift, b * HEADS + head + 1)
                        dve.wait_ge(*L3.filled(("PV", head), b))
                        rows = slice(head % 2 * HDIM, (head % 2 + 1) * HDIM)
                        dve.tensor_tensor(att[rows, :], bank[4][0:HDIM, :], att_lo[0:HDIM, :], ALU.add
                                          ).then_inc(L3.empty(("PV", head)), 1)
                        if head % 2:
                            dve.wait_ge(att_hi, b * PAIRS + head // 2 + 1)
                            dve.tensor_tensor(at3[head // 2 % 2][:, 1, :], att, f32(at3[head // 2 % 2][:, 0, :]),
                                              ALU.subtract).then_inc(at_ready, 1)
                for t in range(2):
                    dve.wait_ge(*L3.filled(("O", t), b))
                    dve.tensor_tensor(y3[:, 2 * t:2 * t + 2, :].rearrange("p a d -> p (a d)"), bank[6 + t][:, :],
                                      xn[:, 2 * t:2 * t + 2, :].rearrange("p a d -> p (a d)"), ALU.add
                                      ).then_inc(L3.empty(("O", t)), 1)

                def row3(k):
                    return rows3[:, k:k + 1, :].to_broadcast([P, NBLK, D])

                for t in range(2):
                    dve.wait_ge(*L3.emptied(("O", t), b))
                link(dve.tensor_tensor(y3, y3, row3(0), ALU.add))
                moments(lambda i: y3[:, i, :])
                dve.wait_ge(rstd_ready, b * 2 + (2 * NSEQ + 2))
                for i in range(NBLK):
                    ins = dve.tensor_scalar(t3[:, i, :], y3[:, i, :], mv[:, i, 0:1], rstd[:, i:i + 1],
                                            ALU.subtract, ALU.mult)
                link(ins)
                link(dve.tensor_tensor(t3, t3, row3(1), ALU.mult))
                link(dve.tensor_tensor(t3, t3, row3(2), ALU.add))
                hb = h[:, bass.ds(b * NBLK, NBLK), :]
                dve.tensor_tensor(hb, t3, hb, ALU.add).then_inc(h3_done, 1)
                steps.end()
            dve.wait_ge(h3_done, NSEQ)

            def quantize(x, n, out_, b_, magnitude_ready):
                nb = n // FPB
                amax, inv, a, c = q_max[:, 0:nb], q_inv[:, 0:nb], q_a[:, 0:n], b_[:, 0:n]
                mid = q_b[:, 0:n]

                def blocks(ap):
                    return ap.rearrange("p (m k) -> p m k", k=FPB)

                def wide(ap):
                    return ap.rearrange("p (m a) -> p m a", a=1).to_broadcast([P, nb, FPB])

                link(dve.tensor_reduce(amax, blocks(x), AX.X, ALU.max, apply_absolute_value=True))
                link(dve.tensor_scalar(amax, amax, 1.0 / 6.0, 1e-12, ALU.mult, ALU.max))
                link(dve.reciprocal(inv, amax))
                link(dve.tensor_scalar(inv, inv, BELOW, None, ALU.mult))
                dve.wait_ge(*magnitude_ready)
                link(dve.tensor_tensor(blocks(a), blocks(a), wide(inv), ALU.mult))
                dve.tensor_scalar(mid, a, 2.0, 4.0, ALU.max, ALU.min)
                link(dve.tensor_scalar(c, a, 2.0, GRID_HALF, ALU.min, ALU.add))
                link(dve.tensor_scalar(mid, mid, GRID_ONE, GRID_ONE, ALU.add, ALU.subtract))
                link(dve.scalar_tensor_tensor(c, c, GRID_HALF, mid, ALU.subtract, ALU.add))
                link(dve.tensor_scalar(mid, a, 4.0, GRID_TWO, ALU.max, ALU.add))
                link(dve.scalar_tensor_tensor(c, mid, GRID_TWO + 6.0, c, ALU.subtract, ALU.add))
                link(dve.tensor_tensor(blocks(c), blocks(c), wide(amax), ALU.mult))
                return dve.scalar_tensor_tensor(out_[:, 0:n].bitcast(U32), x.bitcast(U32), 0x80000000,
                                                c.bitcast(U32), ALU.bitwise_and, ALU.bitwise_or)

            QLINKS = 11
            n_banks = 0
            steps.start(0, QLINKS * len(W4_JOBS))
            for n, (kind, part) in enumerate(W4_JOBS):
                dve.wait_ge(w4_in, 16 * w4_loaded(n))
                w = w4_width(kind, part)
                quantize(q_x[:, 0:w], w, q_c[:, 0, :], q_c[:, 1, :], (w4_abs, n + 1)).then_inc(w4_quantized, 1)
                for _, parts in w4_turns(kind, part, q_c[:, 0, :]):
                    dve.wait_ge(w4_hi, n_banks + 1)
                    for rows, at, cols, dst in parts:
                        ins = dve.tensor_tensor(dst(1), bank[n_banks % 2][0:rows, at:at + cols], f32(dst(0)),
                                                ALU.subtract)
                    ins.then_inc(w4_split, 1)
                    n_banks += 1
            steps.end()
            with dve.Fori(0, NSEQ) as b:
                steps.start(b, 2 + (2 + NBLK) * QLINKS)
                JOBS = 2 + NBLK
                moments(lambda i: h_at(b, i))
                dve.wait_ge(rstd_ready, b + (4 * NSEQ + 1))
                for i in range(NBLK):
                    ins = dve.tensor_scalar(xn[:, i, :], h_at(b, i), mv[:, i, 0:1], rstd[:, i:i + 1],
                                            ALU.subtract, ALU.mult)
                ins.then_inc(to_abs, 1)
                dve.wait_ge(to_abs, b + 1)
                for t in range(2):
                    quantize(x_half(t), 2 * D, x_half(t), q_c[:, 1, :], (abs_ready, b * JOBS + t + 1)
                             ).then_inc(xq_ready, 1)
                x_lo(L4, b, 3 * NSEQ * KD)

                def add_down(i):
                    dve.wait_ge(*L4.filled(("down", i), b))
                    dve.tensor_tensor(h_at(b, i), bank[i % 2][:, 0:D], h_at(b, i), ALU.add
                                      ).then_inc(L4.empty(("down", i)), 1)

                for i in range(NBLK):
                    for t in range(2):
                        cols = slice(t * (FF // 2), (t + 1) * (FF // 2))
                        dve.wait_ge(*L4.filled(("up", i, t), b))
                        dve.wait_ge(*L4.emptied(("gate", i, t), b))
                        dve.tensor_tensor(q_x[:, cols], bank[4 + t][:, 0:FF // 2], silu[:, cols], ALU.mult
                                          ).then_inc(L4.empty(("up", i, t)), 1)
                    dve.wait_ge(*L4.emptied(("up", i, 1), b))
                    quantize(q_x[:, 0:FF], FF, q_c[:, i % 2, :], q_c[:, i % 2, :],
                             (abs_ready, b * JOBS + (3 + i))).then_inc(hq_ready, 1)
                    for t in range(2):
                        dve.wait_ge(*L4.filled(("hT", i, t), b))
                        dve.wait_ge(hT_hi, b * (2 * NBLK) + (2 * i + t + 1))
                        for (dst, src), (hi, _) in zip(h_parts(1, t), h_parts(0, t)):
                            ins = dve.tensor_tensor(dst, src, f32(hi), ALU.subtract)
                        ins.then_inc(L4.empty(("hT", i, t)), 1)
                    if i:
                        add_down(i - 1)
                add_down(NBLK - 1)
                steps.end()


def kernel(x, L0_tok_weight, L0_attn_W_qkva, L0_attn_gamma, L0_ffn_q_node_w, L0_ffn_q_node_b, L0_ffn_q_w1,
           L0_ffn_q_b1, L0_ffn_q_w2, L0_ffn_q_b2, L0_ffn_k_node_w, L0_ffn_k_node_b, L0_ffn_k_w1, L0_ffn_k_b1,
           L0_ffn_k_w2, L0_ffn_k_b2, L0_ffn_v_node_w, L0_ffn_v_node_b, L0_ffn_v_w1, L0_ffn_v_b1, L0_ffn_v_w2,
           L0_ffn_v_b2, L1_attn_adaptive_scale, L1_attn_Wq, L1_attn_bq, L1_attn_Wk, L1_attn_bk, L1_attn_Wv,
           L1_attn_bv, L1_attn_Wo, L1_attn_bo, L1_attn_gamma, L1_attn_beta, L1_ffn_w_gate, L1_ffn_w_up,
           L1_ffn_w_down):
    import numpy as np
    import concourse.bacc as bacc
    from concourse.bass_utils import run_bass_kernel_spmd

    def by_partition(a, chunks):
        a = np.asarray(a)
        return a.reshape(chunks, P, -1).transpose(1, 0, 2).reshape(P, -1)

    def t(a):
        return np.asarray(a).T

    node_w = np.concatenate([np.asarray(a) for a in (L0_ffn_q_node_w, L0_ffn_k_node_w, L0_ffn_v_node_w)])
    node_b = np.concatenate([np.asarray(a) for a in (L0_ffn_q_node_b, L0_ffn_k_node_b, L0_ffn_v_node_b)])
    w2raw = []
    for w1, w2 in ((L0_ffn_q_w1, L0_ffn_q_w2), (L0_ffn_k_w1, L0_ffn_k_w2), (L0_ffn_v_w1, L0_ffn_v_w2)):
        w2raw += [by_partition(np.asarray(w1).transpose(1, 0, 2).reshape(D, HID), KD),
                  by_partition(np.asarray(w2).reshape(HID, D), NH2)]
    route = np.zeros((3, RT, HID), np.float32)
    b2 = np.zeros((RT, 3, D), np.float32)
    for f, b in enumerate((L0_ffn_q_b2, L0_ffn_k_b2, L0_ffn_v_b2)):
        for leaf in range(LEAVES):
            route[f, TREE * f + leaf, leaf * LEAFW:(leaf + 1) * LEAFW] = FAR
        b2[TREE * f:TREE * f + LEAVES, f, :] = np.asarray(b)
    w3raw = np.concatenate([by_partition(t(w), KD) for w in (L1_attn_Wq, L1_attn_Wk, L1_attn_Wv)]
                           + [by_partition(t(L1_attn_Wo), PAIRS)], axis=1)
    scale = np.asarray(L1_attn_adaptive_scale)
    arrays = {
        "ids": np.asarray(x).reshape(NSEQ * NBLK, P).T,
        "table": np.asarray(L0_tok_weight),
        "w1qkva": by_partition(t(L0_attn_W_qkva), KD),
        "gamma1": np.asarray(L0_attn_gamma).reshape(KD, P).T,
        "node_w": by_partition(node_w.T, KD).reshape(P, KD, 3 * NODES),
        "node_b": node_b.reshape(1, -1),
        "w2raw": np.concatenate(w2raw, axis=1),
        "route": route,
        "b1": np.stack([np.asarray(a).reshape(HID) for a in (L0_ffn_q_b1, L0_ffn_k_b1, L0_ffn_v_b1)]),
        "b2": b2,
        "w3raw": w3raw.reshape(P, NCH3, CH).transpose(1, 0, 2),
        "bq": np.asarray(L1_attn_bq).reshape(PAIRS, P).T,
        "bk": np.asarray(L1_attn_bk).reshape(PAIRS, P).T,
        "bv": np.asarray(L1_attn_bv).reshape(HEADS, HDIM).T,
        "ascale_row": scale.reshape(1, HEADS),
        "ascale_part": np.repeat(scale.reshape(PAIRS, 2), HDIM, axis=1).T,
        "bo": np.asarray(L1_attn_bo).reshape(1, D),
        "gamma3": np.asarray(L1_attn_gamma).reshape(1, D),
        "beta3": np.asarray(L1_attn_beta).reshape(1, D),
        "w_gate": np.asarray(L1_ffn_w_gate),
        "w_up": np.asarray(L1_ffn_w_up),
        "w_down": np.asarray(L1_ffn_w_down),
        "ident": np.eye(P, dtype=np.float32),
    }
    nc = bacc.Bacc("TRN2", target_bir_lowering=False, num_devices=1)
    given, args = {}, []
    for name, a in arrays.items():
        a = np.ascontiguousarray(a)
        given[f"in_{name}"] = a
        args.append(nc.dram_tensor(f"in_{name}", a.shape, mybir.dt.from_np(a.dtype), kind="ExternalInput").ap())
    out = nc.dram_tensor("out", (NSEQ, SEQ, D), F32, kind="ExternalOutput").ap()
    build(nc, *args, out)
    got = run_bass_kernel_spmd(nc, [given], core_ids=[0])
    return got.results[0]["out"]
```

```python
from contextlib import ExitStack

import concourse.bass as bass
from concourse import mybir

F32 = mybir.dt.float32
F32R = mybir.dt.float32r
U32 = mybir.dt.uint32
I32 = mybir.dt.int32
ALU = mybir.AluOpType
ACT = mybir.ActivationFunctionType
AX = mybir.AxisListType

P = 128
NSEQ, SEQ, D = 4, 512, 256
NBLK = SEQ // P
KD = D // P
SPLIT = 2

E1 = 3 * D
LEAVES, LEAFW, DEPTH = 16, 64, 4
NODES = LEAVES - 1
HID = LEAVES * LEAFW
NH2 = HID // P
TREE = 32
RT = 3 * TREE
NNODE = 48
FAR = 2.0 ** 120
HEADS, HDIM = 16, 64
PAIRS = HEADS // 2
QUARTERS = 4
UNITS = HEADS * NBLK
FF = 704
FPB = 16
NFB = FF // FPB
FK = (FF + P - 1) // P
FTAIL = FF - (FK - 1) * P
GRID_HALF = 0.75 * 2.0 ** 23
GRID_ONE = 1.5 * 2.0 ** 23
GRID_TWO = 3.0 * 2.0 ** 23
BELOW = 1.0 - 2.0 ** -23

CH = 512
NCH2 = 3 * 4 * 1024 // CH
NCH3 = 8 * 1024 // CH
LN_EPS = 1e-5


class Banks:

    def __init__(self, filled, emptied):
        self.filled_sem, self.emptied_sem = filled, emptied
        self.before = [0] * 8

    def layer(self, order, times=NSEQ):
        if hasattr(self, "place"):
            self.before = [n + self.times * k for n, k in zip(self.before, self.per)]
        self.times = times
        self.place, self.per = {}, [0] * 8
        for what, bank in order:
            assert what not in self.place
            self.place[what] = (bank, self.per[bank])
            self.per[bank] += 1
        return BankLayer(self, dict(self.place), list(self.per), list(self.before))


class BankLayer:
    def __init__(self, banks, place, per, before):
        self.banks, self.place, self.per, self.before = banks, place, per, before

    def count(self, what, b, more):
        bank, n = self.place[what]
        return b * self.per[bank] + (self.before[bank] + n + more)

    def room(self, what, b):
        return self.banks.emptied_sem[self.place[what][0]], self.count(what, b, 1)

    def filled(self, what, b):
        return self.banks.filled_sem[self.place[what][0]], self.count(what, b, 1)

    def emptied(self, what, b):
        return self.banks.emptied_sem[self.place[what][0]], self.count(what, b, 2)

    def fill(self, what):
        return self.banks.filled_sem[self.place[what][0]]

    def empty(self, what):
        return self.banks.emptied_sem[self.place[what][0]]


class Steps:

    def __init__(self, sem):
        self.sem, self.base = sem, 0

    def start(self, b, per):
        self.b, self.per, self.n = b, per, 0

    def end(self):
        assert self.n == self.per, f"steps {self.n}, declared {self.per}"
        self.base += self.per * (NSEQ if self.per and not isinstance(self.b, int) else 1)

    def link(self, eng, ins):
        self.n += 1
        ins.then_inc(self.sem, 1)
        eng.wait_ge(self.sem, self.b * self.per + (self.base + self.n))


def unit_steps():
    pe, act, dve, pool = [], [], [], []
    for u in range(UNITS + 4):
        pair, r = divmod(u, 2 * NBLK)
        ahead = [("S", u + 2)] if u < UNITS else []
        turn = [("T", u)] if u < UNITS else []
        weigh = [("PV", (u - 3) // 2)] if u % 2 and 3 <= u < UNITS + 3 else []
        head = [("PV", (u - 4) // 2)] if u % 4 == 2 and u >= 6 else []
        both = [("pair", (u - 11) // 8)] if u % 8 == 3 and u >= 11 else []

        def products(u):
            pair, r = divmod(u, 2 * NBLK)
            at = {0: ("Q", pair + 1), 2: ("K", pair + 1)}
            if pair % 2:
                at.update({4: ("V", (pair + 1) // 2, 0), 6: ("V", (pair + 1) // 2, 1)})
            late = UNITS - 10
            if u >= late:
                return {late: ("xT", 0), late + 2: ("xT", 1), late + 4: ("Q", PAIRS), late + 6: ("K", PAIRS),
                        late + 8: ("V", QUARTERS, 0), late + 10: ("V", QUARTERS, 1)}.get(u)
            return at.get(r)

        project = [products(u)] if products(u) else []
        lagged = [products(u - 1)] if u and products(u - 1) else []
        if pair % 2 and r == 5:
            project += [("O", pair - 1, 0), ("O", pair - 1, 1)]
        elif pair and pair % 2 == 0 and r in (4, 6) and pair < PAIRS:
            project += [("O", pair - 1, (r - 4) // 2)]
        norm = UNITS - 24
        piece = [("norm", u - norm)] if norm <= u < norm + 11 else []
        pe += ahead + weigh + project + turn
        act += lagged + head + ahead + turn + both
        turned, recip = [("T", u - 1)] if 0 < u <= UNITS else [], [("recip", u + 2)] if ahead else []
        dve += ahead + (lagged + head + recip + turned if lagged or head else turned + recip) + both + piece
        pool += ahead + ([("root",)] if u == norm + 5 else []) + ([("rest", u - 8)] if 8 <= u < 16 else [])
    pe += [("O", PAIRS - 1, 0), ("O", PAIRS - 1, 1)]
    return pe, act, dve, pool


FIRST3 = [("xT", k) for k in range(KD)] + [("Q", 0), ("K", 0), ("V", 0, 0), ("V", 0, 1), ("S", 0), ("S", 1)]


def build(nc, ids, table, w1qkva, gamma1, node_w, node_b, w2raw, route, b1, b2, w3raw, bq, bk, bv,
          ascale_row, ascale_part, bo, gamma3, beta3, w_gate, w_up, w_down, ident_in, out):
    with ExitStack() as ctx:
        def region(name, cols, dt):
            return ctx.enter_context(nc.sbuf_tensor(name, [P, cols], dt))

        def sem(name):
            return ctx.enter_context(nc.semaphore(name))

        opnd = region("operands", 41472, F32R)
        data = region("data", 10240, F32)
        small = region("small", 600, F32)
        idx = region("token_ids", NSEQ * NBLK, I32)

        def cut(tensor, at, *shape):
            n = 1
            for s in shape:
                n *= s
            ap = tensor[:, at:at + n]
            names = "abcd"[:len(shape)]
            if len(shape) == 1:
                return ap
            return ap.rearrange(f"p ({' '.join(names)}) -> p {' '.join(names)}",
                                **{c: s for c, s in zip(names[1:], shape[1:])})

        def f32(ap):
            return ap.bitcast(F32)

        h = cut(data, 0, NSEQ * NBLK, D)
        xn = cut(data, 4096, NBLK, D)
        A0 = 5120
        raw = cut(data, A0 + 2048, 3, CH)
        gate = cut(data, A0, KD, SEQ)
        scan = cut(data, A0 + 1024, KD, SEQ)
        W2 = 0
        w2 = cut(opnd, W2, SPLIT, 3, 4, 1024)
        xT = cut(opnd, 24576, SPLIT, KD, SEQ)
        route_w = cut(opnd, 26624, 3, HID)
        b2w = cut(opnd, 29696, SPLIT, 3, D)
        selT = cut(opnd, 31232, 2, SEQ)
        hid = cut(opnd, 32256, 3, SPLIT, SEQ)
        qT = cut(opnd, 35328, SPLIT, KD, SEQ)
        kT = cut(opnd, 37376, SPLIT, KD, SEQ)
        v2 = cut(opnd, 39424, SPLIT, NBLK, D)
        pT2 = cut(opnd, 32256, 2, SPLIT, SEQ)
        w1 = cut(opnd, 35328, SPLIT, KD, E1)
        route_lo = cut(opnd, 39424, HID)
        p2 = cut(data, A0, 2, SEQ)
        sel = cut(data, A0 + 1024, NBLK, 2, RT)
        path = cut(data, A0 + 1024 + NBLK * 2 * RT, 3, NBLK, 3, 8)
        w3 = cut(opnd, 0, SPLIT, 8, 1024)
        qk = cut(opnd, 32256, 2, 2, SPLIT, SEQ)
        vs = cut(opnd, 36352, 2, NBLK, 4, P)
        pT3 = cut(opnd, 26624, 2, SPLIT, NBLK, D)
        at3 = (cut(opnd, 30720, SPLIT, SEQ), cut(opnd, 40448, SPLIT, SEQ))
        p3 = cut(data, A0, 2, SEQ)
        pn3 = cut(data, A0 + 1024, 2, SEQ)
        att = cut(data, A0 + 2048, SEQ)
        att_lo = cut(data, A0 + 2560, SEQ)
        rawl = cut(data, A0, 4, CH)
        xnext = cut(data, A0 + 3840, NBLK, D)
        h_after = cut(data, 0, NSEQ * NBLK + NBLK, D)
        rows3 = cut(data, A0 + 3072, 3, D)
        wgu = cut(opnd, 0, SPLIT, KD, 2 * FF)
        wdn = cut(opnd, 5632, SPLIT, FK, D)
        hqT = cut(opnd, 8704, SPLIT, FK, P)
        FW = 768
        q_x = data[:, A0:A0 + FW]
        q_a = data[:, A0 + FW:A0 + 2 * FW]
        q_b = data[:, A0 + 2 * FW:A0 + 3 * FW]
        q_c = cut(data, A0 + 3 * FW, 2, FW)
        silu = data[:, A0 + 5 * FW:A0 + 5 * FW + FF]
        q_max = data[:, A0 + 4544:A0 + 4544 + FW // FPB]
        q_inv = data[:, A0 + 4592:A0 + 4592 + FW // FPB]

        ident = small[:, 0:128]
        stats = cut(small, 128, NBLK, 6)
        mv = cut(small, 152, NBLK, 2)
        var_e = small[:, 160:164]
        rstd = small[:, 164:168]
        sdev = small[:, 168:172]
        coef = small[:, 172:176]
        neg_half = small[:, 176:180]
        pos_half = small[:, 180:184]
        gam1 = small[:, 184:186]
        nodeb = small[:, 186:186 + 3 * NODES]
        nodew = cut(small, 240, KD, NNODE)
        score = cut(small, 336, NBLK, 3 * NODES)
        nmax = small[:, 520:524]
        rsum = small[:, 524:528]
        rinv = small[:, 528:532]
        bqs = small[:, 532:540]
        bks = small[:, 540:548]
        bvs = small[:, 548:564]
        asr = small[:, 564:580]
        asp = small[:, 580:588]
        nodeR = region("node_operands", SPLIT * KD * NNODE, F32R)
        noder = cut(nodeR, 0, SPLIT, KD, NNODE)

        bank = [ctx.enter_context(nc.psum_tensor(f"bank{k}", [P, 512], F32)) for k in range(8)]
        banks = Banks([sem(f"bank_filled{k}") for k in range(8)], [sem(f"bank_emptied{k}") for k in range(8)])

        L1 = banks.layer([(("xT", k), k) for k in range(KD)]
                         + [((n, c), 2 + 3 * c + m) for c in range(KD) for m, n in enumerate(("a", "kv", "q"))]
                         + [(("back", t), t) for t in range(2)])
        hid_bank = {(f, j): 5 + (NH2 * f + j) % 3 for f in range(3) for j in range(NH2)}
        order = [(("xT", k), k) for k in range(KD)] + [("node", 2), ("selT", 3), ("takT", 4)]
        for f in range(3):
            order += [(("hid", f, j), hid_bank[f, j]) for j in range(NH2)]
            order += [(("tree", f, o), o) for o in range(KD if f < 2 else NBLK)]
        for i in range(NBLK):
            order += [(("S", i), 4 + i % 2), (("T", i), 6 + i % 2), (("PV", i), i % 2)]
        L2 = banks.layer(order)
        PE_STEPS3, ACT_STEPS3, DVE_STEPS3, POOL_STEPS3 = unit_steps()
        L3first = banks.layer([(s, {"xT": 4, "Q": 5, "K": 2, "V": 3, "S": 0}[s[0]] + (s[-1] if s[0] in ("xT", "V", "S") else 0))
                               for s in FIRST3], 1)
        order = []
        for s in PE_STEPS3:
            if s[0] == "PV":
                if s[1] % 2 == 0:
                    order.append((("PV", s[1] // 2), 4))
            elif s[0] == "O":
                if s[1] == PAIRS - 1:
                    order.append((("O", s[2]), 6 + s[2]))
            else:
                order.append((s, {"S": s[1] % 2, "T": 2 + s[1] % 2}.get(s[0], 5)))
        L3 = banks.layer(order)
        order = [(("xT", k), k) for k in range(KD)]
        for i in range(NBLK):
            order += [(("gate", i, t), 2 + t) for t in range(2)] + [(("up", i, t), 4 + t) for t in range(2)]
            order += [(("hT", i, t), 6 + t) for t in range(2)] + [(("down", i), i % 2)]
        L4 = banks.layer(order)

        ids_in = sem("ids_in")
        consts_in = sem("consts_in")
        rows_gathered = sem("rows_gathered")
        w1_in = sem("w1_in")
        route_in = sem("route_in")
        route_lo_moved = sem("route_lo_moved")
        raw_in = [sem(f"raw_in{s}") for s in range(4)]
        raw_hi = sem("raw_hi")
        raw_lo = sem("raw_lo")
        w1_ready = sem("w1_ready")
        setup_done = sem("setup_done")
        route_split = sem("route_split")
        var_ready = sem("var_ready")
        rstd_ready = sem("rstd_ready")
        xn_ready = sem("xn_ready")
        xhi_ready = sem("xhi_ready")
        gate_ready = sem("gate_ready")
        sel_ready = sem("sel_ready")
        hid_hi = sem("hid_hi")
        hid_used = sem("hid_used")
        tree_hi = sem("tree_hi")
        nmax_ready = sem("nmax_ready")
        p_hi = sem("p_hi")
        dve_step = sem("dve_step")
        pool_step = sem("pool_step")
        w3_prepared = sem("w3_prepared")
        rows3_in = sem("rows3_in")
        proj_hi = sem("proj_hi")
        rinv_ready = sem("rinv_ready")
        pn_ready = sem("pn_ready")
        att_shift = sem("att_shift")
        att_ready = sem("att_ready")
        att_hi = sem("att_hi")
        at_ready = sem("at_ready")
        w3_prepared_q = sem("w3_prepared_q")
        w3_hi = sem("w3_hi")
        coef_ready = sem("coef_ready")
        h3_done = sem("h3_done")
        w4_in = sem("w4_in")
        w4_abs = sem("w4_abs")
        w4_quantized = sem("w4_quantized")
        w4_turned = sem("w4_turned")
        w4_hi = sem("w4_hi")
        w4_split = sem("w4_split")
        to_abs = sem("to_abs")
        abs_ready = sem("abs_ready")
        xq_ready = sem("xq_ready")
        hq_ready = sem("hq_ready")
        hT_hi = sem("hT_hi")
        stored = sem("stored")

        block = ctx.enter_context(nc.Block())

        out_rows = out.rearrange("b (i p) d -> p (b i) d", p=P)

        W4_JOBS = [("gate", (0, 3)), ("gate", (3, 5)), ("up", (0, 3)), ("up", (3, 5)), ("tails", None),
                   ("down", 0), ("down", 1)]

        def w4_width(kind, part):
            return {"tails": D, "down": FF}.get(kind) or (part[1] - part[0]) * D

        def w4_loads(kind, part):
            if kind in ("gate", "up"):
                n0, n1 = part
                w = w_gate if kind == "gate" else w_up
                return [(q_x[:, 0:(n1 - n0) * D].rearrange("p (n k) -> p n k", k=D),
                         w[n0 * P:n1 * P, :].rearrange("(n p) k -> p n k", p=P))]
            if kind == "tails":
                return [(q_x[0:FTAIL, 0:D], w_gate[5 * P:FF, :]), (q_x[FTAIL:P, 0:D], w_up[5 * P:FF, :])]
            return [(q_x[:, 0:FF], w_down[part * P:(part + 1) * P, :])]

        def w4_loaded(n):
            return sum(2 if kind == "tails" else 1 for kind, _ in W4_JOBS[:n + 1])

        def w4_turns(kind, part, q):
            if kind in ("gate", "up"):
                n0, n1 = part
                m = 0 if kind == "gate" else FF
                return [([(q[:, (n - n0) * D + k * P:(n - n0) * D + (k + 1) * P], (n - n0) * P, P)
                          for n in range(n0, n1)],
                         [(P, 0, (n1 - n0) * P, lambda s, k=k: wgu[:, s, k, m + n0 * P:m + n1 * P])])
                        for k in range(KD)]
            if kind == "tails":
                return [([(q[:, k * P:(k + 1) * P], 0, P)],
                         [(P, m * FTAIL, FTAIL, lambda s, k=k, m=m: wgu[:, s, k, m * FF + 5 * P:(m + 1) * FF])
                          for m in range(2)]) for k in range(KD)]
            cols = slice(part * P, (part + 1) * P)
            return [([(q[:, c * P:c * P + (P if c < FK - 1 else FTAIL)], c % 3 * P, P if c < FK - 1 else FTAIL)
                      for c in range(3 * t, 3 * t + 3)],
                     [(P, c % 3 * P, P, lambda s, c=c: wdn[:, s, c, cols]) if c < FK - 1 else
                      (FTAIL, c % 3 * P, P, lambda s, c=c: wdn[0:FTAIL, s, c, cols])
                      for c in range(3 * t, 3 * t + 3)]) for t in range(2)]

        def w2_flat(part):
            return cut(opnd, W2 + part * 3 * 4 * 1024, 3 * 4 * 1024)

        def w3_flat(part):
            return cut(opnd, part * 8 * 1024, 8 * 1024)

        def x_half(t):
            return xn[:, 2 * t:2 * t + 2, :].rearrange("p a d -> p (a d)")

        def h_parts(part, t):
            for rows, c0, c1 in ((P, 0, 3),) if t == 0 else ((P, 3, 5), (FTAIL, 5, 6)):
                yield (hqT[0:rows, part, c0:c1, :],
                       bank[6 + t][0:rows, (c0 - 3 * t) * P:(c1 - 3 * t) * P].rearrange("p (c q) -> p c q", q=P))

        def tree_out(act, f, b):
            for o in range(KD if f < 2 else NBLK):
                act.wait_ge(*L2.filled(("tree", f, o), b))
                if f < 2:
                    act.activation((qT, kT)[f][:, 0, o, :], bank[o][:, :], ACT.Copy,
                                   scale=D ** -0.5 if f == 0 else 1.0).then_inc(tree_hi, 1)
                else:
                    act.activation(v2[:, 0, o, :], bank[o][:, 0:D], ACT.Copy).then_inc(tree_hi, 1)

        @block.sync
        def _(sp):
            sp.dma_start(idx[:, :], ids).then_inc(ids_in, 16)
            sp.dma_start(raw.rearrange("p a b -> p (a b)"), w1qkva).then_inc(w1_in, 16)
            sp.wait_ge(setup_done, 3)
            for dst, src in ((ident, ident_in), (gam1, gamma1), (nodew[:, :, 0:3 * NODES], node_w),
                             (nodeb, node_b.to_broadcast([P, 3 * NODES])), (bqs, bq), (bks, bk),
                             (asp, ascale_part), (asr, ascale_row.to_broadcast([P, HEADS])),
                             (bvs[64:128, :], bv)):
                sp.dma_start(dst, src).then_inc(consts_in, 16)
            for f in range(3):
                rows = TREE * f
                sp.dma_start(scan.rearrange("p a b -> p (a b)")[0:RT, :], route[f]).then_inc(route_in, 16)
                sp.wait_ge(route_in, 16 * (3 * f + 1))
                for r in range(2):
                    sp.dma_start(scan.rearrange("p a b -> p (a b)")[rows + LEAVES + r:rows + LEAVES + r + 1, :],
                                 b1[f:f + 1, :]).then_inc(route_in, 16)
                sp.wait_ge(route_split, f + 1)
                row = TREE * f + LEAVES + 1
                sp.dma_start(f32(route_w[row:row + 1, f, :]), f32(route_lo[row:row + 1, :])).then_inc(route_lo_moved, 16)
                sp.wait_ge(route_lo_moved, 16 * (f + 1))
            sp.dma_start(cut(data, A0, 3, D)[0:RT], b2).then_inc(consts_in, 16)
            sp.wait_ge(w1_ready, 2)
            with sp.Fori(0, NSEQ) as b:
                for k in range(6):
                    sp.wait_ge(raw_lo, b * 6 + k + 1)
                    sp.dma_start(raw[:, k % 3, :], w2raw[:, bass.ds(b * (6 * CH) + k * CH, CH)]
                                 ).then_inc(raw_in[k % 3], 16)
            for k in range(NCH3):
                if k < 4:
                    sp.wait_ge(*L2.emptied(("PV", 3), NSEQ - 1))
                    if k == 0:
                        sp.wait_ge(*L2.emptied(("PV", 2), NSEQ - 1))
                else:
                    sp.wait_ge(w3_prepared, k - 4 + 1)
                sp.dma_start(rawl[:, k % 4, :], w3raw[k]).then_inc(raw_in[k % 4], 16)
            for k, src in enumerate((bo, gamma3, beta3)):
                sp.dma_start(rows3[:, k, :], src.to_broadcast([P, D])).then_inc(rows3_in, 16)
            sp.wait_ge(h3_done, NSEQ)
            for n, (kind, part) in enumerate(W4_JOBS):
                if n:
                    sp.wait_ge(w4_quantized, n)
                for dst, src in w4_loads(kind, part):
                    sp.dma_start(dst, src).then_inc(w4_in, 16)
            with sp.Fori(0, NSEQ) as b:
                sp.wait_ge(*L4.emptied(("down", 2), b))
                sp.wait_ge(*L4.emptied(("down", 3), b))
                sp.dma_start(out_rows[:, bass.ds(b * NBLK, NBLK), :], h[:, bass.ds(b * NBLK, NBLK), :]
                             ).then_inc(stored, 16)
            sp.wait_ge(stored, 16 * NSEQ)

        @block.gpsimd
        def _(pool):
            pool.memset(neg_half, -0.5).then_inc(setup_done, 1)
            pool.memset(pos_half, 0.5).then_inc(setup_done, 1)
            pool.wait_ge(ids_in, 16)
            pool.wait_ge(setup_done, 3)

            def root(b, dst, src, exponent):
                return pool.tensor_tensor(dst, src, exponent, ALU.pow)

            for n in range(NSEQ * NBLK):
                pool.indirect_dma_start(h[:, n, :], None, table,
                                        bass.IndirectOffsetOnAxis(ap=idx[:, n:n + 1].bitcast(U32), axis=0)
                                        ).then_inc(rows_gathered, 16)
            with pool.Fori(0, NSEQ) as b:
                pool.wait_ge(var_ready, b + 1)
                root(b, sdev, mv[:, :, 1], pos_half)
                root(b, rstd, var_e, neg_half).then_inc(rstd_ready, 1)
                for k in range(6):
                    pool.wait_ge(raw_hi, b * 6 + k + 1)
                    at = bass.ds(b * 6 * CH + k * CH, CH)
                    pool.tensor_tensor(w2_flat(1)[:, at], raw[:, k % 3, :], f32(w2_flat(0)[:, at]),
                                       ALU.subtract).then_inc(raw_lo, 1)
            with pool.Fori(0, NSEQ) as b:
                pool.wait_ge(var_ready, b + (NSEQ + 1))
                root(b, rstd, var_e, neg_half).then_inc(rstd_ready, 1)
            pool.wait_ge(var_ready, 2 * NSEQ + 1)
            root(0, rstd, var_e, neg_half).then_inc(rstd_ready, 1)

            def weights(u, b):
                pool.wait_ge(rinv_ready, b * UNITS + (u + 1))
                if u >= 2:
                    pool.wait_ge(*L3.filled(("T", u - 2), b))
                pool.sem_inc(pool_step, 1)
                pool.tensor_scalar(pn3[:, u % 2, :], p3[:, u % 2, :], rinv[:, u % 4:u % 4 + 1], 1.0,
                                   ALU.mult, ALU.mult).then_inc(pn_ready, 1)

            weights(0, 0)
            weights(1, 0)
            with pool.Fori(0, NSEQ) as b:
                for s_ in POOL_STEPS3:
                    if s_[0] == "S":
                        weights(s_[1], b)
                    elif s_[0] == "root":
                        pool.wait_ge(var_ready, b * 2 + (2 * NSEQ + 2))
                        root(b, rstd, var_e, neg_half).then_inc(rstd_ready, 1)
                    elif s_[1] < NBLK:
                        pool.tensor_tensor(xn[:, s_[1], :], xnext[:, s_[1], :], rows3[:, 0, :], ALU.add)
                    else:
                        hb = h[:, bass.ds(b * NBLK + (s_[1] - NBLK), 1), :].rearrange("p a d -> p (a d)")
                        pool.tensor_tensor(hb, hb, rows3[:, 2, :], ALU.add)
                pool.wait_ge(var_ready, b * 2 + (2 * NSEQ + 3))
                root(b, rstd, var_e, neg_half).then_inc(rstd_ready, 1)
            with pool.Fori(0, NSEQ) as b:
                pool.wait_ge(var_ready, b + (4 * NSEQ + 2))
                root(b, rstd, var_e, neg_half).then_inc(rstd_ready, 1)

        @block.tensor
        def _(pe):
            def product(dst, stat, mov, start, stop, **kw):
                pe.matmul(dst, stat(0), mov(0), start=start, stop=False, **kw)
                pe.matmul(dst, stat(0), mov(1), start=False, stop=False, **kw)
                return pe.matmul(dst, stat(1), mov(0), start=False, stop=stop, **kw)

            def turn_x(L, b, ready, base, per=NBLK):
                for k in range(KD):
                    pe.wait_ge(*L.room(("xT", k), b))
                for i in range(NBLK):
                    if i % (NBLK // per) == 0:
                        pe.wait_ge(ready, b * per + (base + i // (NBLK // per) + 1))
                    for k in range(KD):
                        mm = pe.transpose(bank[L.place[("xT", k)][0]][:, i * P:(i + 1) * P],
                                          xn[:, i, k * P:(k + 1) * P], ident)
                        if i == NBLK - 1:
                            mm.then_inc(L.fill(("xT", k)), 1)

            pe.wait_ge(consts_in, 16 * 10)
            pe.wait_ge(w1_ready, 2)
            with pe.Fori(0, NSEQ) as b:
                turn_x(L1, b, xn_ready, 0)
                for k in range(KD):
                    pe.wait_ge(*L1.emptied(("xT", k), b))
                for c in range(KD):
                    for what, e in (("a", 2 * KD + c), ("kv", KD + c), ("q", c)):
                        pe.wait_ge(*L1.room((what, c), b))
                        dst = bank[L1.place[(what, c)][0]]
                        for k in range(KD):
                            mm = product(dst[:, :], lambda s: w1[:, s, k, e * P:(e + 1) * P],
                                         lambda s: xT[:, s, k, :], k == 0, k == KD - 1)
                        mm.then_inc(L1.fill((what, c)), 1)
                for t in range(2):
                    pe.wait_ge(*L1.room(("back", t), b))
                for c in range(KD):
                    pe.wait_ge(*L1.emptied(("q", c), b))
                    for i in range(NBLK):
                        mm = pe.transpose(bank[i // 2][:, i % 2 * D + c * P:i % 2 * D + (c + 1) * P],
                                          scan[:, c, i * P:(i + 1) * P], ident)
                        if c == KD - 1 and i % 2:
                            mm.then_inc(L1.fill(("back", i // 2)), 1)
            pe.wait_ge(raw_lo, 3 + NCH2)
            pe.wait_ge(route_lo_moved, 48)
            with pe.Fori(0, NSEQ) as b:
                turn_x(L2, b, xn_ready, NSEQ * NBLK)
                for k in range(KD):
                    pe.wait_ge(*L2.emptied(("xT", k), b))
                pe.wait_ge(*L2.room("node", b))
                for i in range(NBLK):
                    for k in range(KD):
                        mm = product(bank[2][:, i * 64:i * 64 + NNODE], lambda s: xT[:, s, k, i * P:(i + 1) * P],
                                     lambda s: noder[:, s, k, :], k == 0, k == KD - 1)
                mm.then_inc(L2.fill("node"), 1)

                def w1_block(f, j):
                    what = ("hid", f, j)
                    pe.wait_ge(*L2.room(what, b))
                    dst = bank[hid_bank[f, j]][:, :]
                    cols = slice(j * P, (j + 1) * P)
                    for k in range(KD):
                        product(dst, lambda s: w2[:, s, f, k, cols], lambda s: xT[:, s, k, :], k == 0, False)
                    if (f, j) == (0, 0):
                        route_rows()
                    pe.matmul(dst, route_w[0:RT, f, cols], selT[0:RT, 0, :], start=False, stop=True
                              ).then_inc(L2.fill(what), 1)

                def route_rows():
                    pe.wait_ge(*L2.room("selT", b))
                    pe.wait_ge(*L2.room("takT", b))
                    pe.wait_ge(sel_ready, b + 1)
                    for s, what in ((0, "selT"), (1, "takT")):
                        for i in range(NBLK):
                            mm = pe.transpose(bank[3 + s][0:RT, i * P:(i + 1) * P], sel[:, i, s, :], ident)
                        mm.then_inc(L2.fill(what), 1)
                    pe.wait_ge(*L2.emptied("selT", b))
                    pe.wait_ge(*L2.emptied("takT", b))

                def w2_block(f, j):
                    slot = (NH2 * f + j) % 3
                    pe.wait_ge(*L2.emptied(("hid", f, j), b))
                    w2j = lambda s: w2[:, s, f, 2 + j // 4, j % 4 * D:(j % 4 + 1) * D]
                    for o in range(KD if f < 2 else NBLK):
                        cols = slice(o * P, (o + 1) * P)
                        if j == 0:
                            pe.wait_ge(*L2.room(("tree", f, o), b))
                        if f < 2:
                            dst = bank[o][:, :]
                            if j == 0:
                                pe.matmul(dst, b2w[0:RT, 0, f, cols], selT[0:RT, 1, :], start=True, stop=False)
                                pe.matmul(dst, b2w[0:RT, 1, f, cols], selT[0:RT, 1, :], start=False, stop=False)
                            mm = product(dst, lambda s: w2j(s)[:, cols], lambda s: hid[:, slot, s, :],
                                         False, j == NH2 - 1)
                        else:
                            dst = bank[o][:, 0:D]
                            if j == 0:
                                pe.matmul(dst, selT[0:RT, 1, cols], b2w[0:RT, 0, f, :], start=True, stop=False)
                                pe.matmul(dst, selT[0:RT, 1, cols], b2w[0:RT, 1, f, :], start=False, stop=False)
                            mm = product(dst, lambda s: hid[:, slot, s, cols], w2j, False, j == NH2 - 1)
                        if j == NH2 - 1:
                            mm.then_inc(L2.fill(("tree", f, o)), 1)

                seq = [(f, j) for f in range(3) for j in range(NH2)]
                for n in range(len(seq) + 2):
                    if n < len(seq):
                        w1_block(*seq[n])
                    if n >= 2:
                        w2_block(*seq[n - 2])

                def scores(i):
                    pe.wait_ge(*L2.room(("S", i), b))
                    if i == 0:
                        for f in range(2):
                            for o in range(KD):
                                pe.wait_ge(*L2.emptied(("tree", f, o), b))
                    for k in range(KD):
                        mm = product(bank[4 + i % 2][:, :], lambda s: qT[:, s, k, i * P:(i + 1) * P],
                                     lambda s: kT[:, s, k, :], k == 0, k == KD - 1)
                    mm.then_inc(L2.fill(("S", i)), 1)

                def turn_p(i):
                    pe.wait_ge(*L2.room(("T", i), b))
                    pe.wait_ge(*L2.emptied(("S", i), b))
                    for kb in range(NBLK):
                        mm = pe.transpose(bank[6 + i % 2][:, kb * P:(kb + 1) * P], p2[:, i % 2, kb * P:(kb + 1) * P],
                                          ident)
                    mm.then_inc(L2.fill(("T", i)), 1)

                def weigh(i):
                    pe.wait_ge(*L2.room(("PV", i), b))
                    if i == 0:
                        for o in range(NBLK):
                            pe.wait_ge(*L2.emptied(("tree", 2, o), b))
                    pe.wait_ge(*L2.emptied(("T", i), b))
                    for kb in range(NBLK):
                        mm = product(bank[i % 2][:, 0:D], lambda s: pT2[:, i % 2, s, kb * P:(kb + 1) * P],
                                     lambda s: v2[:, s, kb, :], kb == 0, kb == NBLK - 1)
                    mm.then_inc(L2.fill(("PV", i)), 1)

                scores(0)
                scores(1)
                for i in range(NBLK):
                    turn_p(i)
                    if i + 2 < NBLK:
                        scores(i + 2)
                    weigh(i)
            pe.wait_ge(w3_prepared, NCH3)
            def step3(s_, L, b, first):
                what = s_[0]
                if what == "xT":
                    k = s_[1]
                    pe.wait_ge(*L.room(s_, b))
                    pe.wait_ge(xn_ready, b * NBLK + (2 * NSEQ + (1 if first else 2)) * NBLK)
                    for i in range(NBLK):
                        mm = pe.transpose(bank[L.place[s_][0]][:, i * P:(i + 1) * P],
                                          xnext[:, i, k * P:(k + 1) * P], ident)
                    mm.then_inc(L.fill(s_), 1)
                elif what in ("Q", "K"):
                    pair = s_[1] % PAIRS
                    if what == "Q" and s_[1] in (0, PAIRS):
                        for k in range(KD):
                            pe.wait_ge(*L.emptied(("xT", k), b))
                    pe.wait_ge(*L.room(s_, b))
                    m = 2 * (what == "K")
                    for k in range(KD):
                        mm = product(bank[L.place[s_][0]][:, :], lambda s: w3[:, s, m + k, pair * P:(pair + 1) * P],
                                     lambda s: xT[:, s, k, :], k == 0, k == KD - 1)
                    mm.then_inc(L.fill(s_), 1)
                elif what == "V":
                    _, quarter, t = s_
                    quarter = quarter % QUARTERS
                    pe.wait_ge(*L.room(s_, b))
                    for kb in (2 * t, 2 * t + 1):
                        for k in range(KD):
                            mm = product(bank[L.place[s_][0]][:, kb % 2 * D:kb % 2 * D + D],
                                         lambda s: xT[:, s, k, kb * P:(kb + 1) * P],
                                         lambda s: w3[:, s, 4 + k, quarter * D:(quarter + 1) * D],
                                         k == 0, k == KD - 1)
                    mm.then_inc(L.fill(s_), 1)
                elif what == "S":
                    u = s_[1]
                    head, i = divmod(u, NBLK)
                    pair, rows = head // 2, slice(head % 2 * HDIM, head % 2 * HDIM + HDIM)
                    if u % (2 * NBLK) == 0:
                        if first:
                            pe.wait_ge(*L.emptied(("Q", 0), b))
                        pe.wait_ge(*L.emptied(("K", pair), b))
                    pe.wait_ge(*L.room(s_, b))
                    product(bank[u % 2][:, :], lambda s: qk[rows, pair % 2, 0, s, i * P:(i + 1) * P],
                            lambda s: qk[rows, pair % 2, 1, s, :], True, True).then_inc(L.fill(s_), 1)
                elif what == "T":
                    u = s_[1]
                    pe.wait_ge(*L.room(s_, b))
                    pe.wait_ge(pn_ready, b * UNITS + u + 1)
                    for kb in range(NBLK):
                        mm = pe.transpose(bank[2 + u % 2][:, kb * P:(kb + 1) * P],
                                          pn3[:, u % 2, kb * P:(kb + 1) * P], ident)
                    mm.then_inc(L.fill(s_), 1)
                elif what == "PV":
                    head, half = divmod(s_[1], 2)
                    if half == 0:
                        pe.wait_ge(*L.room(("PV", head), b))
                    if head % 4 == 0 and half == 0 and head:
                        pe.wait_ge(*L.emptied(("V", head // 4, 1), b))
                    pe.wait_ge(*L.emptied(("T", 2 * s_[1]), b))
                    pe.wait_ge(*L.emptied(("T", 2 * s_[1] + 1), b))
                    for kb in range(NBLK):
                        for s in range(SPLIT):
                            mm = pe.matmul(bank[4][:, half * D:(half + 1) * D],
                                           vs[:, head // 4 % 2, kb, head % 4, :], pT3[:, half, s, kb, :],
                                           start=(kb == 0 and s == 0), stop=(kb == NBLK - 1 and s == 1))
                    if half == 1:
                        mm.then_inc(L.fill(("PV", head)), 1)
                elif what == "O":
                    _, pair, t = s_
                    if pair == 0:
                        pe.wait_ge(*L.room(("O", t), b))
                    pe.wait_ge(at_ready, b * PAIRS + pair + 1)
                    for i in (2 * t, 2 * t + 1):
                        mm = product(bank[6 + i // 2][:, i % 2 * D:(i % 2 + 1) * D],
                                     lambda s: at3[pair % 2][:, s, i * P:(i + 1) * P],
                                     lambda s: w3[:, s, 6 + pair // 4, pair % 4 * D:(pair % 4 + 1) * D],
                                     pair == 0 and i % 2 == 0, pair == PAIRS - 1, skip_group_check=True)
                        if pair == PAIRS - 1 and i % 2:
                            mm.then_inc(L.fill(("O", i // 2)), 1)
            for s_ in FIRST3:
                step3(s_, L3first, 0, True)
            with pe.Fori(0, NSEQ) as b:
                for s_ in PE_STEPS3:
                    step3(s_, L3, b, False)
            n_banks = 0
            for n, (kind, part) in enumerate(W4_JOBS):
                pe.wait_ge(w4_quantized, n + 1)
                for turns, _ in w4_turns(kind, part, q_c[:, 0, :]):
                    if n_banks >= 2:
                        pe.wait_ge(w4_split, n_banks - 1)
                    for src, at, rows in turns:
                        mm = pe.transpose(bank[n_banks % 2][0:rows, at:at + P], src, ident)
                    mm.then_inc(w4_turned, 1)
                    n_banks += 1
            pe.wait_ge(w4_split, n_banks)
            with pe.Fori(0, NSEQ) as b:
                turn_x(L4, b, xq_ready, 0, 2)
                for k in range(KD):
                    pe.wait_ge(*L4.emptied(("xT", k), b))

                def gate_up(i):
                    for m, what in enumerate(("gate", "up")):
                        for t in range(2):
                            pe.wait_ge(*L4.room((what, i, t), b))
                            lo = m * FF + t * (FF // 2)
                            for k in range(KD):
                                mm = product(bank[2 + 2 * m + t][:, 0:FF // 2],
                                             lambda s: xT[:, s, k, i * P:(i + 1) * P],
                                             lambda s: wgu[:, s, k, lo:lo + FF // 2], k == 0, k == KD - 1)
                            mm.then_inc(L4.fill((what, i, t)), 1)

                def turn_h(i):
                    pe.wait_ge(hq_ready, b * NBLK + i + 1)
                    for t in range(2):
                        pe.wait_ge(*L4.room(("hT", i, t), b))
                        for c in range(3 * t, 3 * t + 3):
                            rows = P if c < FK - 1 else FTAIL
                            mm = pe.transpose(bank[6 + t][0:rows, c % 3 * P:c % 3 * P + P],
                                              q_c[:, i % 2, c * P:c * P + rows], ident)
                        mm.then_inc(L4.fill(("hT", i, t)), 1)

                def down(i):
                    pe.wait_ge(*L4.room(("down", i), b))
                    for t in range(2):
                        pe.wait_ge(*L4.emptied(("hT", i, t), b))
                    for c in range(FK):
                        rows = P if c < FK - 1 else FTAIL
                        mm = product(bank[i % 2][:, 0:D], lambda s: hqT[0:rows, s, c, :],
                                     lambda s: wdn[0:rows, s, c, :], c == 0, c == FK - 1)
                    mm.then_inc(L4.fill(("down", i)), 1)

                gate_up(0)
                for i in range(NBLK):
                    if i + 1 < NBLK:
                        gate_up(i + 1)
                    turn_h(i)
                    down(i)

        @block.scalar
        def _(act):
            def x_hi_part(L, b, base, k, scale=None):
                act.wait_ge(*L.filled(("xT", k), b))
                src = bank[L.place[("xT", k)][0]][:, :]
                if scale is None:
                    ins = act.activation(xT[:, 0, k, :], src, ACT.Copy)
                else:
                    ins = act.activation(xT[:, 0, k, :], src, ACT.Identity, scale=scale[:, k:k + 1])
                ins.then_inc(xhi_ready, 1)

            def x_hi(L, b, base, scale=None):
                for k in range(KD):
                    x_hi_part(L, b, base, k, scale)

            act.wait_ge(w1_in, 16)
            act.activation(w1[:, 0, :, :].rearrange("p a b -> p (a b)"), raw.rearrange("p a b -> p (a b)"),
                           ACT.Copy).then_inc(w1_ready, 1)
            act.wait_ge(consts_in, 16 * 10)
            with act.Fori(0, NSEQ) as b:
                x_hi(L1, b, 0, gam1)
                for c in range(KD):
                    act.wait_ge(*L1.filled(("a", c), b))
                    act.activation(gate[:, c, :], bank[L1.place[("a", c)][0]][:, :], ACT.Sigmoid
                                   ).then_inc(L1.empty(("a", c)), 1)
                for k in range(6):
                    act.wait_ge(raw_in[k % 3], b * 32 + 16 * (k // 3 + 1))
                    act.activation(w2_flat(0)[:, bass.ds(b * 6 * CH + k * CH, CH)], raw[:, k % 3, :], ACT.Copy
                                   ).then_inc(raw_hi, 1)
            with act.Fori(0, NSEQ) as b:
                x_hi(L2, b, NSEQ * KD)
                for s, what in ((0, "selT"), (1, "takT")):
                    act.wait_ge(*L2.filled(what, b))
                    act.activation(selT[0:RT, s, :], bank[3 + s][0:RT, :], ACT.Copy).then_inc(L2.empty(what), 1)
                for f in range(3):
                    for j in range(NH2):
                        n = NH2 * f + j
                        act.wait_ge(*L2.filled(("hid", f, j), b))
                        act.activation(hid[:, n % 3, 0, :], bank[hid_bank[f, j]][:, :], ACT.Relu
                                       ).then_inc(hid_hi, 1)
                        if f and j == 1:
                            tree_out(act, f - 1, b)
                tree_out(act, 2, b)

                def exps(i):
                    act.wait_ge(nmax_ready, b * NBLK + i + 1)
                    act.activation(p2[:, i % 2, :], bank[4 + i % 2][:, :], ACT.Exp, bias=nmax[:, i:i + 1],
                                   accum_out=rsum[:, i:i + 1]).then_inc(L2.empty(("S", i)), 1)

                exps(0)
                exps(1)
                for i in range(NBLK):
                    act.wait_ge(*L2.filled(("T", i), b))
                    act.activation(pT2[:, i % 2, 0, :], bank[6 + i % 2][:, :], ACT.Copy).then_inc(p_hi, 1)
                    if i + 2 < NBLK:
                        exps(i + 2)
            def hi3(s_, L, b, first):
                what = s_[0]
                if what == "xT":
                    x_hi_part(L, b, (2 * NSEQ + (0 if first else 1)) * KD, s_[1])
                elif what in ("Q", "K"):
                    pair, m = s_[1] % PAIRS, int(what == "K")
                    act.wait_ge(*L.filled(s_, b))
                    act.activation(qk[:, pair % 2, m, 0, :], bank[L.place[s_][0]][:, :], ACT.Identity,
                                   bias=(bks if m else bqs)[:, pair:pair + 1]).then_inc(proj_hi, 1)
                elif what == "V":
                    _, quarter, t = s_
                    act.wait_ge(*L.filled(s_, b))
                    act.activation(vs[:, quarter % 2, 2 * t:2 * t + 2, :, 0:HDIM],
                                   bank[L.place[s_][0]][:, :].rearrange("p (a g d) -> p a g d", a=2, g=4), ACT.Copy
                                   ).then_inc(proj_hi, 1)
                elif what == "S":
                    u = s_[1]
                    act.wait_ge(nmax_ready, b * UNITS + (NSEQ * NBLK + u + 1))
                    if u >= 2:
                        act.wait_ge(pn_ready, b * UNITS + (u - 1))
                    act.activation(p3[:, u % 2, :], bank[u % 2][:, :], ACT.Exp, bias=nmax[:, u % 4:u % 4 + 1],
                                   accum_out=rsum[:, u % 4:u % 4 + 1]).then_inc(L.empty(s_), 1)
                elif what == "T":
                    u = s_[1]
                    act.wait_ge(*L.filled(s_, b))
                    act.activation(pT3[:, u // 2 % 2, 0, :, u % 2 * P:(u % 2 + 1) * P],
                                   bank[2 + u % 2][:, :].rearrange("p (k q) -> p k q", k=NBLK), ACT.Copy
                                   ).then_inc(p_hi, 1)
                elif what == "PV":
                    head = s_[1] // 2
                    act.wait_ge(*L.filled(("PV", head), b))
                    act.activation(att_lo[0:HDIM, :], bank[4][HDIM:P, :], ACT.Identity,
                                   bias=bvs[HDIM:P, head:head + 1]).then_inc(att_shift, 1)
                elif what == "pair":
                        head = 2 * s_[1] + 1
                        act.wait_ge(*L.emptied(("PV", head), b))
                        act.activation(at3[head // 2 % 2][:, 0, :], att, ACT.Copy).then_inc(att_hi, 1)

            for k in range(NCH3):
                if k < 4:
                    act.wait_ge(w3_prepared_q, k + 1)
                else:
                    act.wait_ge(raw_in[k % 4], (0 if k % 4 == 3 else 16 * 2 * NSEQ) + 16 * (k // 4 + 1))
                act.activation(w3_flat(0)[:, k * CH:(k + 1) * CH], rawl[:, k % 4, :], ACT.Copy
                               ).then_inc(w3_hi, 1)
            for s_ in FIRST3:
                hi3(s_, L3first, 0, True)
            with act.Fori(0, NSEQ) as b:
                for s_ in ACT_STEPS3:
                    hi3(s_, L3, b, False)
            n_banks = 0
            for n, (kind, part) in enumerate(W4_JOBS):
                act.wait_ge(w4_in, 16 * w4_loaded(n))
                if n:
                    act.wait_ge(w4_quantized, n)
                w = w4_width(kind, part)
                act.activation(q_a[:, 0:w], q_x[:, 0:w], ACT.Abs).then_inc(w4_abs, 1)
                for _, parts in w4_turns(kind, part, q_c[:, 0, :]):
                    act.wait_ge(w4_turned, n_banks + 1)
                    for rows, at, cols, dst in parts:
                        ins = act.activation(dst(0), bank[n_banks % 2][0:rows, at:at + cols], ACT.Copy)
                    ins.then_inc(w4_hi, 1)
                    n_banks += 1
            with act.Fori(0, NSEQ) as b:
                def magnitude(src):
                    act.activation(q_a[:, 0:src.shape[1]], src, ACT.Abs).then_inc(abs_ready, 1)

                act.wait_ge(to_abs, b + 1)
                magnitude(x_half(0))
                act.wait_ge(xq_ready, b * 2 + 1)
                magnitude(x_half(1))
                x_hi(L4, b, (3 * NSEQ + 1) * KD)
                for i in range(NBLK):
                    for t in range(2):
                        act.wait_ge(*L4.filled(("gate", i, t), b))
                        act.activation(silu[:, t * (FF // 2):(t + 1) * (FF // 2)], bank[2 + t][:, 0:FF // 2],
                                       ACT.Silu).then_inc(L4.empty(("gate", i, t)), 1)
                    act.wait_ge(*L4.emptied(("up", i, 1), b))
                    magnitude(q_x[:, 0:FF])
                    for t in range(2):
                        act.wait_ge(*L4.filled(("hT", i, t), b))
                        for dst, src in h_parts(0, t):
                            ins = act.activation(dst, src, ACT.Copy)
                        ins.then_inc(hT_hi, 1)

        @block.vector
        def _(dve):
            steps = Steps(dve_step)

            def link(ins):
                steps.link(dve, ins)

            for k in range(8):
                dve.sem_inc(banks.emptied_sem[k], 1)
            dve.sem_inc(raw_lo, 3)

            def moments(src):
                for i in range(NBLK):
                    ins = dve.bn_stats(stats[:, i, :], src(i))
                link(ins)
                dve.memset(var_e, 0.0)
                for i in range(NBLK):
                    ins = dve.bn_aggr(mv[:, i, :], stats[:, i, :])
                link(ins)
                dve.tensor_scalar(var_e, mv[:, :, 1], LN_EPS, None, ALU.add).then_inc(var_ready, 1)

            def h_at(b, i, n=1):
                ap = h[:, bass.ds(b * NBLK + i, n), :]
                return ap.rearrange("p a d -> p (a d)")

            def normalize(b, mult, done):
                for i in range(NBLK):
                    dve.tensor_scalar(xn[:, i, :], h_at(b, i), mv[:, i, 0:1], mult[:, i:i + 1],
                                      ALU.subtract, ALU.mult).then_inc(done, 1)

            def x_lo_part(L, b, base, k, scale=None):
                dve.wait_ge(*L.filled(("xT", k), b))
                dve.wait_ge(xhi_ready, b * KD + (base + k + 1))
                src = bank[L.place[("xT", k)][0]][:, :]
                if scale is None:
                    ins = dve.tensor_tensor(xT[:, 1, k, :], src, f32(xT[:, 0, k, :]), ALU.subtract)
                else:
                    ins = dve.scalar_tensor_tensor(xT[:, 1, k, :], src, scale[:, k:k + 1],
                                                   f32(xT[:, 0, k, :]), ALU.mult, ALU.subtract)
                ins.then_inc(L.empty(("xT", k)), 1)

            def x_lo(L, b, base, scale=None):
                for k in range(KD):
                    x_lo_part(L, b, base, k, scale)

            steps.start(0, 4)
            dve.memset(nodew, 0.0).then_inc(setup_done, 1)
            dve.wait_ge(w1_in, 16)
            dve.wait_ge(w1_ready, 1)
            dve.tensor_tensor(w1[:, 1, :, :].rearrange("p a b -> p (a b)"), raw.rearrange("p a b -> p (a b)"),
                              f32(w1[:, 0, :, :].rearrange("p a b -> p (a b)")), ALU.subtract).then_inc(w1_ready, 1)
            for f in range(3):
                dve.wait_ge(route_in, 16 * 3 * (f + 1))
                src = scan.rearrange("p a b -> p (a b)")[0:RT, :]
                link(dve.tensor_copy(route_w[0:RT, f, :], src))
                if f:
                    dve.wait_ge(route_lo_moved, 16 * f)
                dve.tensor_tensor(route_lo[0:RT, :], src, f32(route_w[0:RT, f, :]), ALU.subtract
                                  ).then_inc(route_split, 1)
            dve.wait_ge(consts_in, 16 * 10)
            b2s = cut(data, A0, 3, D)[0:RT]
            dve.tensor_copy(noder[:, 0, :, :], nodew)
            link(dve.tensor_copy(b2w[0:RT, 0, :, :], b2s))
            dve.tensor_tensor(noder[:, 1, :, :], nodew, f32(noder[:, 0, :, :]), ALU.subtract)
            dve.tensor_tensor(b2w[0:RT, 1, :, :], b2s, f32(b2w[0:RT, 0, :, :]), ALU.subtract)
            steps.end()
            dve.wait_ge(rows_gathered, 16 * NSEQ * NBLK)
            with dve.Fori(0, NSEQ) as b:
                steps.start(b, 5)
                moments(lambda i: h_at(b, i))
                dve.wait_ge(rstd_ready, b + 1)
                link(dve.scalar_tensor_tensor(coef, sdev, D ** 0.5, rstd, ALU.mult, ALU.mult))
                link(dve.tensor_scalar(coef, coef, 1e-12, None, ALU.max))
                link(dve.reciprocal(coef, coef))
                dve.scalar_tensor_tensor(coef, coef, D ** 0.5, rstd, ALU.mult, ALU.mult).then_inc(coef_ready, 1)
                dve.wait_ge(coef_ready, b + 1)
                normalize(b, coef, xn_ready)
                x_lo(L1, b, 0, gam1)
                for c in range(KD):
                    dve.wait_ge(*L1.filled(("kv", c), b))
                    dve.wait_ge(*L1.emptied(("a", c), b))
                    dve.tensor_tensor_scan(scan[:, c, :], gate[:, c, :], bank[L1.place[("kv", c)][0]][:, :], 0.0,
                                           ALU.mult, ALU.add).then_inc(L1.empty(("kv", c)), 1)
                    dve.wait_ge(*L1.filled(("q", c), b))
                    dve.wait_ge(*L1.emptied(("kv", c), b))
                    dve.tensor_tensor(scan[:, c, :], bank[L1.place[("q", c)][0]][:, :], scan[:, c, :], ALU.mult
                                      ).then_inc(L1.empty(("q", c)), 1)
                for t in range(2):
                    dve.wait_ge(*L1.filled(("back", t), b))
                    dve.tensor_tensor(h_at(b, 2 * t, 2), bank[t][:, :], h_at(b, 2 * t, 2), ALU.add
                                      ).then_inc(L1.empty(("back", t)), 1)
                steps.end()
            for t in range(2):
                dve.wait_ge(*L1.emptied(("back", t), NSEQ - 1))
            steps.start(0, 2)
            link(dve.memset(sel.rearrange("p a b c -> p (a b c)"), 0.0))
            for f in range(3):
                ins = dve.memset(sel[:, :, 0, TREE * f + LEAVES:TREE * f + LEAVES + 2], 1.0)
            link(ins)
            steps.end()
            with dve.Fori(0, NSEQ) as b:
                steps.start(b, 11)
                moments(lambda i: h_at(b, i))
                dve.wait_ge(rstd_ready, b + (NSEQ + 1))
                normalize(b, rstd, xn_ready)
                x_lo(L2, b, NSEQ * KD)
                dve.wait_ge(*L2.filled("node", b))
                dve.tensor_tensor(score, bank[2][:, 0:NBLK * 64].rearrange("p (i n) -> p i n", n=64)[:, :, 0:3 * NODES],
                                  nodeb.rearrange("p (a n) -> p a n", a=1).to_broadcast([P, NBLK, 3 * NODES]),
                                  ALU.add).then_inc(L2.empty("node"), 1)
                dve.wait_ge(*L2.emptied("node", b))
                link(dve.tensor_scalar(score, score, 0.0, None, ALU.is_ge))
                g = score.rearrange("p i (f n) -> p i f n", f=3)
                for level in range(DEPTH):
                    n = 2 ** level
                    gl = g[:, :, :, n - 1:2 * n - 1]
                    if level < DEPTH - 1:
                        kids = path[:, level, :, :, 0:2 * n].rearrange("p i f (n c) -> p i f n c", c=2)
                        left, right = kids[:, :, :, :, 0], kids[:, :, :, :, 1]
                    else:
                        kids = sel[:, :, 1, :].rearrange("p i (f n) -> p i f n", f=3)[:, :, :, 0:LEAVES].rearrange(
                            "p i f (n c) -> p i f n c", c=2)
                        left, right = kids[:, :, :, :, 0], kids[:, :, :, :, 1]
                    if level == 0:
                        dve.tensor_scalar(left, gl, -1.0, 1.0, ALU.mult, ALU.add)
                        link(dve.tensor_copy(right, gl))
                    else:
                        up = path[:, level - 1, :, :, 0:n]
                        link(dve.tensor_tensor(right, up, gl, ALU.mult))
                        link(dve.tensor_tensor(left, up, right, ALU.subtract))
                dve.tensor_scalar(sel[:, :, 0, :].rearrange("p i (f n) -> p i f n", f=3)[:, :, :, 0:LEAVES],
                                  sel[:, :, 1, :].rearrange("p i (f n) -> p i f n", f=3)[:, :, :, 0:LEAVES],
                                  -1.0, None, ALU.add).then_inc(sel_ready, 1)

                def tree_lo(f):
                    for o in range(KD if f < 2 else NBLK):
                        n = KD * f + o
                        dve.wait_ge(*L2.filled(("tree", f, o), b))
                        dve.wait_ge(tree_hi, b * (2 * KD + NBLK) + n + 1)
                        if f == 0:
                            ins = dve.scalar_tensor_tensor(qT[:, 1, o, :], bank[o][:, :], D ** -0.5,
                                                           f32(qT[:, 0, o, :]), ALU.mult, ALU.subtract)
                        elif f == 1:
                            ins = dve.tensor_tensor(kT[:, 1, o, :], bank[o][:, :], f32(kT[:, 0, o, :]), ALU.subtract)
                        else:
                            ins = dve.tensor_tensor(v2[:, 1, o, :], bank[o][:, 0:D], f32(v2[:, 0, o, :]),
                                                    ALU.subtract)
                        ins.then_inc(L2.empty(("tree", f, o)), 1)

                for f in range(3):
                    for j in range(NH2):
                        n = NH2 * f + j
                        dve.wait_ge(*L2.filled(("hid", f, j), b))
                        dve.wait_ge(hid_hi, b * (3 * NH2) + n + 1)
                        dve.scalar_tensor_tensor(hid[:, n % 3, 1, :], bank[hid_bank[f, j]][:, :], 0.0,
                                                 f32(hid[:, n % 3, 0, :]), ALU.max, ALU.subtract
                                                 ).then_inc(L2.empty(("hid", f, j)), 1)
                        if f and j == 1:
                            tree_lo(f - 1)
                tree_lo(2)

                def row_max(i):
                    dve.wait_ge(*L2.filled(("S", i), b))
                    dve.tensor_reduce(nmax[:, i:i + 1], bank[4 + i % 2][:, :], AX.X, ALU.max, negate=True
                                      ).then_inc(nmax_ready, 1)

                def add_out(i):
                    dve.wait_ge(*L2.filled(("PV", i), b))
                    dve.scalar_tensor_tensor(h_at(b, i), bank[i % 2][:, 0:D], rinv[:, i:i + 1], h_at(b, i),
                                             ALU.mult, ALU.add).then_inc(L2.empty(("PV", i)), 1)

                row_max(0)
                row_max(1)
                for i in range(NBLK):
                    dve.wait_ge(*L2.emptied(("S", i), b))
                    ins = dve.reciprocal(rinv[:, i:i + 1], rsum[:, i:i + 1])
                    if i == NBLK - 1:
                        link(ins)
                    dve.wait_ge(*L2.filled(("T", i), b))
                    dve.wait_ge(p_hi, b * NBLK + i + 1)
                    dve.tensor_tensor(pT2[:, i % 2, 1, :], bank[6 + i % 2][:, :], f32(pT2[:, i % 2, 0, :]),
                                      ALU.subtract).then_inc(L2.empty(("T", i)), 1)
                    if i + 2 < NBLK:
                        row_max(i + 2)
                    if i:
                        dve.wait_ge(*L2.emptied(("T", i), b))
                        add_out(i - 1)
                add_out(NBLK - 1)
                steps.end()
            for i in (2, 3):
                dve.wait_ge(*L2.emptied(("PV", i), NSEQ - 1))
            steps.start(0, 2)
            dve.tensor_scalar(asr, asr, HDIM ** -0.5, None, ALU.mult)
            link(dve.tensor_scalar(asp, asp, HDIM ** -0.5, None, ALU.mult))
            link(dve.tensor_tensor(bqs, bqs, asp, ALU.mult))
            steps.end()
            for k in range(4):
                dve.wait_ge(raw_in[k % 4], (0 if k % 4 == 3 else 16 * 2 * NSEQ) + 16)
                heads = slice((k % 2) * CH // HDIM, (k % 2 + 1) * CH // HDIM)
                piece = rawl[:, k, :].rearrange("p (g d) -> p g d", d=HDIM)
                dve.tensor_tensor(piece, piece, asr[:, heads].rearrange("p (g a) -> p g a", a=1).to_broadcast(
                    [P, CH // HDIM, HDIM]), ALU.mult).then_inc(w3_prepared_q, 1)
            for k in range(NCH3):
                dve.wait_ge(w3_hi, k + 1)
                dve.wait_ge(raw_in[k % 4], (0 if k % 4 == 3 else 16 * 2 * NSEQ) + 16 * (k // 4 + 1))
                if k == 0:
                    dve.wait_ge(w3_prepared_q, 4)
                dve.tensor_tensor(w3_flat(1)[:, k * CH:(k + 1) * CH], rawl[:, k % 4, :],
                                  f32(w3_flat(0)[:, k * CH:(k + 1) * CH]), ALU.subtract).then_inc(w3_prepared, 1)
            dve.wait_ge(w3_prepared, NCH3)
            dve.wait_ge(rows3_in, 48)
            first3 = [s_ for s_ in FIRST3 if s_[0] in "QKV"]
            proj3 = [s_ for s_ in DVE_STEPS3 if s_[0] in ("Q", "K", "V")]

            def lo3(s_, L, b, first):
                what = s_[0]
                if what == "xT":
                    x_lo_part(L, b, (2 * NSEQ + (0 if first else 1)) * KD, s_[1])
                elif what in ("Q", "K"):
                    pair, m = s_[1] % PAIRS, int(what == "K")
                    dve.wait_ge(*L.filled(s_, b))
                    dve.wait_ge(proj_hi, b * len(proj3) + (first3.index(s_) + 1 if first else len(first3) + proj3.index(s_) + 1))
                    dve.scalar_tensor_tensor(qk[:, pair % 2, m, 1, :], bank[L.place[s_][0]][:, :],
                                             (bks if m else bqs)[:, pair:pair + 1], f32(qk[:, pair % 2, m, 0, :]),
                                             ALU.add, ALU.subtract).then_inc(L.empty(s_), 1)
                elif what == "V":
                    _, quarter, t = s_
                    dve.wait_ge(*L.filled(s_, b))
                    dve.wait_ge(proj_hi, b * len(proj3) + (first3.index(s_) + 1 if first else len(first3) + proj3.index(s_) + 1))
                    dst = vs[:, quarter % 2, 2 * t:2 * t + 2, :, :]
                    src = bank[L.place[s_][0]][:, :].rearrange("p (a g d) -> p a g d", a=2, g=4)
                    dve.tensor_tensor(dst[:, :, :, HDIM:P], src, f32(dst[:, :, :, 0:HDIM]), ALU.subtract
                                      ).then_inc(L.empty(s_), 1)
                elif what == "S":
                    u = s_[1]
                    dve.wait_ge(*L.filled(s_, b))
                    dve.tensor_reduce(nmax[:, u % 4:u % 4 + 1], bank[u % 2][:, :], AX.X, ALU.max, negate=True
                                      ).then_inc(nmax_ready, 1)
                elif what == "recip":
                    u = s_[1]
                    dve.wait_ge(*L.emptied(("S", u), b))
                    dve.reciprocal(rinv[:, u % 4:u % 4 + 1], rsum[:, u % 4:u % 4 + 1]).then_inc(rinv_ready, 1)
                elif what == "norm":
                    n = s_[1]
                    i, blk_ = n % NBLK, h_after[:, bass.ds(b * NBLK + (NBLK + (n if n < NBLK else n - 7)), 1), :]
                    blk_ = blk_.rearrange("p a d -> p (a d)")
                    if n < NBLK:
                        dve.bn_stats(stats[:, n, :], blk_)
                    elif n == NBLK:
                        for i in range(NBLK):
                            ins = dve.bn_aggr(mv[:, i, :], stats[:, i, :])
                        link(ins)
                        dve.tensor_scalar(var_e, mv[:, :, 1], LN_EPS, None, ALU.add).then_inc(var_ready, 1)
                    elif n >= 7:
                        i = n - 7
                        if i == 0:
                            dve.wait_ge(rstd_ready, b * 2 + (2 * NSEQ + 2))
                        dve.tensor_scalar(xnext[:, i, :], blk_, mv[:, i, 0:1], rstd[:, i:i + 1],
                                          ALU.subtract, ALU.mult).then_inc(xn_ready, 1)
                elif what == "T":
                    u = s_[1]
                    dve.wait_ge(*L.filled(s_, b))
                    dve.wait_ge(p_hi, b * UNITS + (NSEQ * NBLK + u + 1))
                    half = pT3[:, u // 2 % 2, :, :, u % 2 * P:(u % 2 + 1) * P]
                    dve.tensor_tensor(half[:, 1], bank[2 + u % 2][:, :].rearrange("p (k q) -> p k q", k=NBLK),
                                      f32(half[:, 0]), ALU.subtract).then_inc(L.empty(s_), 1)
                elif what == "PV":
                    head = s_[1] // 2
                    dve.wait_ge(att_shift, b * HEADS + head + 1)
                    dve.wait_ge(*L.filled(("PV", head), b))
                    rows = slice(head % 2 * HDIM, (head % 2 + 1) * HDIM)
                    dve.tensor_tensor(att[rows, :], bank[4][0:HDIM, :], att_lo[0:HDIM, :], ALU.add
                                      ).then_inc(L.empty(("PV", head)), 1)
                elif what == "pair":
                        head = 2 * s_[1] + 1
                        dve.wait_ge(att_hi, b * PAIRS + head // 2 + 1)
                        dve.tensor_tensor(at3[head // 2 % 2][:, 1, :], att, f32(at3[head // 2 % 2][:, 0, :]),
                                          ALU.subtract).then_inc(at_ready, 1)

            steps.start(0, 2)
            moments(lambda i: h[:, i, :])
            steps.end()
            dve.wait_ge(rstd_ready, 2 * NSEQ + 1)
            for i in range(NBLK):
                dve.tensor_scalar(xnext[:, i, :], h[:, i, :], mv[:, i, 0:1], rstd[:, i:i + 1],
                                  ALU.subtract, ALU.mult).then_inc(xn_ready, 1)
            for s_ in FIRST3 + [("recip", 0), ("recip", 1)]:
                lo3(s_, L3first, 0, True)
            with dve.Fori(0, NSEQ) as b:
                steps.start(b, 1 + 2 + 1)
                for s_ in DVE_STEPS3:
                    lo3(s_, L3, b, False)
                for t in range(2):
                    dve.wait_ge(*L3.filled(("O", t), b))
                    x2 = xn[:, 2 * t:2 * t + 2, :].rearrange("p a d -> p (a d)")
                    dve.tensor_tensor(x2, bank[6 + t][:, :], x2, ALU.add).then_inc(L3.empty(("O", t)), 1)
                for t in range(2):
                    dve.wait_ge(*L3.emptied(("O", t), b))
                moments(lambda i: xn[:, i, :])
                for i in range(NBLK):
                    ins = dve.scalar_tensor_tensor(xn[:, i, :], xn[:, i, :], mv[:, i, 0:1], rows3[:, 1, :],
                                                   ALU.subtract, ALU.mult)
                link(ins)
                dve.wait_ge(rstd_ready, b * 2 + (2 * NSEQ + 3))
                for i in range(NBLK):
                    ins = dve.scalar_tensor_tensor(h_at(b, i), xn[:, i, :], rstd[:, i:i + 1], h_at(b, i),
                                                   ALU.mult, ALU.add)
                ins.then_inc(h3_done, 1)
                steps.end()
            dve.wait_ge(h3_done, NSEQ)

            def quantize(x, n, out_, b_, magnitude_ready):
                nb = n // FPB
                amax, inv, a, c = q_max[:, 0:nb], q_inv[:, 0:nb], q_a[:, 0:n], b_[:, 0:n]
                mid = q_b[:, 0:n]

                def blocks(ap):
                    return ap.rearrange("p (m k) -> p m k", k=FPB)

                def wide(ap):
                    return ap.rearrange("p (m a) -> p m a", a=1).to_broadcast([P, nb, FPB])

                link(dve.tensor_reduce(amax, blocks(x), AX.X, ALU.max, apply_absolute_value=True))
                link(dve.tensor_scalar(amax, amax, 1.0 / 6.0, 1e-12, ALU.mult, ALU.max))
                link(dve.reciprocal(inv, amax))
                link(dve.tensor_scalar(inv, inv, BELOW, None, ALU.mult))
                dve.wait_ge(*magnitude_ready)
                link(dve.tensor_tensor(blocks(a), blocks(a), wide(inv), ALU.mult))
                dve.tensor_scalar(mid, a, 2.0, 4.0, ALU.max, ALU.min)
                link(dve.tensor_scalar(c, a, 2.0, GRID_HALF, ALU.min, ALU.add))
                link(dve.tensor_scalar(mid, mid, GRID_ONE, GRID_ONE, ALU.add, ALU.subtract))
                link(dve.scalar_tensor_tensor(c, c, GRID_HALF, mid, ALU.subtract, ALU.add))
                link(dve.tensor_scalar(mid, a, 4.0, GRID_TWO, ALU.max, ALU.add))
                link(dve.scalar_tensor_tensor(c, mid, GRID_TWO + 6.0, c, ALU.subtract, ALU.add))
                link(dve.tensor_tensor(blocks(c), blocks(c), wide(amax), ALU.mult))
                return dve.scalar_tensor_tensor(out_[:, 0:n].bitcast(U32), x.bitcast(U32), 0x80000000,
                                                c.bitcast(U32), ALU.bitwise_and, ALU.bitwise_or)

            QLINKS = 11
            n_banks = 0
            steps.start(0, QLINKS * len(W4_JOBS))
            for n, (kind, part) in enumerate(W4_JOBS):
                dve.wait_ge(w4_in, 16 * w4_loaded(n))
                w = w4_width(kind, part)
                quantize(q_x[:, 0:w], w, q_c[:, 0, :], q_c[:, 1, :], (w4_abs, n + 1)).then_inc(w4_quantized, 1)
                for _, parts in w4_turns(kind, part, q_c[:, 0, :]):
                    dve.wait_ge(w4_hi, n_banks + 1)
                    for rows, at, cols, dst in parts:
                        ins = dve.tensor_tensor(dst(1), bank[n_banks % 2][0:rows, at:at + cols], f32(dst(0)),
                                                ALU.subtract)
                    ins.then_inc(w4_split, 1)
                    n_banks += 1
            steps.end()
            with dve.Fori(0, NSEQ) as b:
                steps.start(b, 2 + (2 + NBLK) * QLINKS)
                JOBS = 2 + NBLK
                moments(lambda i: h_at(b, i))
                dve.wait_ge(rstd_ready, b + (4 * NSEQ + 2))
                for i in range(NBLK):
                    ins = dve.tensor_scalar(xn[:, i, :], h_at(b, i), mv[:, i, 0:1], rstd[:, i:i + 1],
                                            ALU.subtract, ALU.mult)
                ins.then_inc(to_abs, 1)
                dve.wait_ge(to_abs, b + 1)
                for t in range(2):
                    quantize(x_half(t), 2 * D, x_half(t), q_c[:, 1, :], (abs_ready, b * JOBS + t + 1)
                             ).then_inc(xq_ready, 1)
                x_lo(L4, b, (3 * NSEQ + 1) * KD)

                def add_down(i):
                    dve.wait_ge(*L4.filled(("down", i), b))
                    dve.tensor_tensor(h_at(b, i), bank[i % 2][:, 0:D], h_at(b, i), ALU.add
                                      ).then_inc(L4.empty(("down", i)), 1)

                for i in range(NBLK):
                    for t in range(2):
                        cols = slice(t * (FF // 2), (t + 1) * (FF // 2))
                        dve.wait_ge(*L4.filled(("up", i, t), b))
                        dve.wait_ge(*L4.emptied(("gate", i, t), b))
                        dve.tensor_tensor(q_x[:, cols], bank[4 + t][:, 0:FF // 2], silu[:, cols], ALU.mult
                                          ).then_inc(L4.empty(("up", i, t)), 1)
                    dve.wait_ge(*L4.emptied(("up", i, 1), b))
                    quantize(q_x[:, 0:FF], FF, q_c[:, i % 2, :], q_c[:, i % 2, :],
                             (abs_ready, b * JOBS + (3 + i))).then_inc(hq_ready, 1)
                    for t in range(2):
                        dve.wait_ge(*L4.filled(("hT", i, t), b))
                        dve.wait_ge(hT_hi, b * (2 * NBLK) + (2 * i + t + 1))
                        for (dst, src), (hi, _) in zip(h_parts(1, t), h_parts(0, t)):
                            ins = dve.tensor_tensor(dst, src, f32(hi), ALU.subtract)
                        ins.then_inc(L4.empty(("hT", i, t)), 1)
                    if i:
                        add_down(i - 1)
                add_down(NBLK - 1)
                steps.end()


def kernel(x, L0_tok_weight, L0_attn_W_qkva, L0_attn_gamma, L0_ffn_q_node_w, L0_ffn_q_node_b, L0_ffn_q_w1,
           L0_ffn_q_b1, L0_ffn_q_w2, L0_ffn_q_b2, L0_ffn_k_node_w, L0_ffn_k_node_b, L0_ffn_k_w1, L0_ffn_k_b1,
           L0_ffn_k_w2, L0_ffn_k_b2, L0_ffn_v_node_w, L0_ffn_v_node_b, L0_ffn_v_w1, L0_ffn_v_b1, L0_ffn_v_w2,
           L0_ffn_v_b2, L1_attn_adaptive_scale, L1_attn_Wq, L1_attn_bq, L1_attn_Wk, L1_attn_bk, L1_attn_Wv,
           L1_attn_bv, L1_attn_Wo, L1_attn_bo, L1_attn_gamma, L1_attn_beta, L1_ffn_w_gate, L1_ffn_w_up,
           L1_ffn_w_down):
    import numpy as np
    import concourse.bacc as bacc
    from concourse.bass_utils import run_bass_kernel_spmd

    def by_partition(a, chunks):
        a = np.asarray(a)
        return a.reshape(chunks, P, -1).transpose(1, 0, 2).reshape(P, -1)

    def t(a):
        return np.asarray(a).T

    node_w = np.concatenate([np.asarray(a) for a in (L0_ffn_q_node_w, L0_ffn_k_node_w, L0_ffn_v_node_w)])
    node_b = np.concatenate([np.asarray(a) for a in (L0_ffn_q_node_b, L0_ffn_k_node_b, L0_ffn_v_node_b)])
    w2raw = []
    for w1, w2 in ((L0_ffn_q_w1, L0_ffn_q_w2), (L0_ffn_k_w1, L0_ffn_k_w2), (L0_ffn_v_w1, L0_ffn_v_w2)):
        w2raw += [by_partition(np.asarray(w1).transpose(1, 0, 2).reshape(D, HID), KD),
                  by_partition(np.asarray(w2).reshape(HID, D), NH2)]
    route = np.zeros((3, RT, HID), np.float32)
    b2 = np.zeros((RT, 3, D), np.float32)
    for f, b in enumerate((L0_ffn_q_b2, L0_ffn_k_b2, L0_ffn_v_b2)):
        for leaf in range(LEAVES):
            route[f, TREE * f + leaf, leaf * LEAFW:(leaf + 1) * LEAFW] = FAR
        b2[TREE * f:TREE * f + LEAVES, f, :] = np.asarray(b)
    w3raw = np.concatenate([by_partition(t(w), KD) for w in (L1_attn_Wq, L1_attn_Wk, L1_attn_Wv)]
                           + [by_partition(t(L1_attn_Wo), PAIRS)], axis=1)
    scale = np.asarray(L1_attn_adaptive_scale)
    arrays = {
        "ids": np.asarray(x).reshape(NSEQ * NBLK, P).T,
        "table": np.asarray(L0_tok_weight),
        "w1qkva": by_partition(t(L0_attn_W_qkva), KD),
        "gamma1": np.asarray(L0_attn_gamma).reshape(KD, P).T,
        "node_w": by_partition(node_w.T, KD).reshape(P, KD, 3 * NODES),
        "node_b": node_b.reshape(1, -1),
        "w2raw": np.concatenate(w2raw, axis=1),
        "route": route,
        "b1": np.stack([np.asarray(a).reshape(HID) for a in (L0_ffn_q_b1, L0_ffn_k_b1, L0_ffn_v_b1)]),
        "b2": b2,
        "w3raw": w3raw.reshape(P, NCH3, CH).transpose(1, 0, 2),
        "bq": np.asarray(L1_attn_bq).reshape(PAIRS, P).T,
        "bk": np.asarray(L1_attn_bk).reshape(PAIRS, P).T,
        "bv": np.asarray(L1_attn_bv).reshape(HEADS, HDIM).T,
        "ascale_row": scale.reshape(1, HEADS),
        "ascale_part": np.repeat(scale.reshape(PAIRS, 2), HDIM, axis=1).T,
        "bo": np.asarray(L1_attn_bo).reshape(1, D),
        "gamma3": np.asarray(L1_attn_gamma).reshape(1, D),
        "beta3": np.asarray(L1_attn_beta).reshape(1, D),
        "w_gate": np.asarray(L1_ffn_w_gate),
        "w_up": np.asarray(L1_ffn_w_up),
        "w_down": np.asarray(L1_ffn_w_down),
        "ident": np.eye(P, dtype=np.float32),
    }
    nc = bacc.Bacc("TRN2", target_bir_lowering=False, num_devices=1)
    given, args = {}, []
    for name, a in arrays.items():
        a = np.ascontiguousarray(a)
        given[f"in_{name}"] = a
        args.append(nc.dram_tensor(f"in_{name}", a.shape, mybir.dt.from_np(a.dtype), kind="ExternalInput").ap())
    out = nc.dram_tensor("out", (NSEQ, SEQ, D), F32, kind="ExternalOutput").ap()
    build(nc, *args, out)
    got = run_bass_kernel_spmd(nc, [given], core_ids=[0])
    return got.results[0]["out"]
```
